# Optimizing a Trainium2 kernel written in Bass

```python
import numpy as np
import jax
import jax.numpy as jnp

def _softmax(x, axis=-1):
    return jax.nn.softmax(x, axis=axis)

def _gelu(x):
    return jax.nn.gelu(x, approximate=True)

def _silu(x):
    return jax.nn.silu(x)

def _sigmoid(x):
    return jax.nn.sigmoid(x)

def _layernorm(x, axis=-1, eps=1e-05):
    m = jnp.mean(x, axis=axis, keepdims=True)
    v = jnp.var(x, axis=axis, keepdims=True)
    return (x - m) / jnp.sqrt(v + eps)

def _scatter_add(tgt, idx, src, axis=0):
    return tgt.at[idx].add(src)

def _segment_sum(src, seg, n):
    return jax.ops.segment_sum(src, seg, n)
kernel_name = 'mk_xattn_ffn_d1_seqx_r8_a43367'

def setup_inputs(seed: int=0):
    np.random.seed(seed)
    _w = jnp.asarray

    def _rec_inputs():
        import jax
        import jax.numpy as jnp
        _rk = jax.random.key(seed)
        x = 7.22e-05 + 1 * jax.random.normal(jax.random.fold_in(_rk, 1), (64, 128, 128), jnp.float32)
        _lenS = 128 - jax.random.randint(jax.random.fold_in(_rk, 7), (64,), 0, max(1, 128 // 4) + 1, jnp.int32)
        _lenS2 = 77 - jax.random.randint(jax.random.fold_in(_rk, 8), (64,), 0, max(1, 77 // 4) + 1, jnp.int32)
        _ctx_1024P = jax.random.normal(jax.random.fold_in(_rk, 11), (64, 16, 128), jnp.float32)
        _ctx_1024c = jax.random.dirichlet(jax.random.fold_in(_rk, 511), 0.3 * jnp.ones((16,), jnp.float32), (64, 77))
        _ctx_1024t = jnp.einsum('bsk,bkd->bsd', _ctx_1024c, _ctx_1024P)
        _ctx_1024t = _ctx_1024t * jax.lax.rsqrt(jnp.mean(jnp.square(_ctx_1024t)) + 1e-12) * 0.953939
        ctx_1024 = 0.00191187 + 0.999416 * (_ctx_1024t + 0.3 * jax.random.normal(jax.random.fold_in(_rk, 611), (64, 77, 128), jnp.float32))
        return (x, ctx_1024)
    x, ctx_1024 = _rec_inputs()

    def _L0_xattn_setup():
        import jax, jax.numpy as jnp
        import numpy as np
        EPS = 1e-06

        def _rmsnorm(x, w, eps=EPS):
            x32 = x.astype(jnp.float32)
            var = jnp.mean(x32 * x32, axis=-1, keepdims=True)
            return (x32 * jax.lax.rsqrt(var + eps)).astype(x.dtype) * w
        key = jax.random.key(seed)
        ks = jax.random.split(key, 6)
        B, S, K, H = (4, 256, 64, 128)
        return {'hidden_states': jax.random.normal(ks[0], (B, S, H), jnp.float32), 'memory_state': jax.random.normal(ks[1], (B, K, H), jnp.float32), 'q_w': jax.random.normal(ks[2], (H, H), jnp.float32) * (1.0 / np.sqrt(H)), 'k_w': jax.random.normal(ks[3], (H, H), jnp.float32) * (1.0 / np.sqrt(H)), 'norm_w': jnp.ones((H,), jnp.float32), 'gate_w': jax.random.normal(ks[4], (H, H), jnp.float32) * 0.02, 'gate_b': jnp.zeros((H,), jnp.float32)}
    _L0_xattn_all = _L0_xattn_setup()
    _L0_xattn_in = {k: v for k, v in _L0_xattn_all.items() if k in ('q_w', 'k_w', 'norm_w', 'gate_w', 'gate_b')}
    del _L0_xattn_all

    def _L0_ffn_setup():
        import jax, jax.numpy as jnp
        import numpy as np
        D = 128
        E = 8
        H = 256
        TOP_K = 2
        ALPHA = 0.5
        LN_EPS = 1e-05

        def _experts_all(x, W1, b1, W2, b2):
            h = jax.nn.relu(jnp.einsum('bld,edh->eblh', x, W1) + b1[:, None, None, :])
            return jnp.einsum('eblh,ehd->ebld', h, W2) + b2[:, None, None, :]

        def _selected_expert(x, expert_idx, W1, b1, W2, b2):
            oh = jax.nn.one_hot(expert_idx, E, dtype=x.dtype)
            return jnp.einsum('ebld,ble->bld', _experts_all(x, W1, b1, W2, b2), oh)

        def _layer_norm(x, gamma, beta):
            mu = jnp.mean(x, axis=-1, keepdims=True)
            var = jnp.mean(jnp.square(x - mu), axis=-1, keepdims=True)
            return (x - mu) * jax.lax.rsqrt(var + LN_EPS) * gamma + beta
        key = jax.random.key(seed)
        ks = jax.random.split(key, 8)
        x = jax.random.normal(ks[0], (2, 256, D), dtype=jnp.float32)
        gate_W = jax.random.normal(ks[1], (D, E), dtype=jnp.float32) * 0.02
        gate_b = jnp.zeros((E,), dtype=jnp.float32)
        W1 = jax.random.normal(ks[2], (E, D, H), dtype=jnp.float32) * 0.02
        b1 = jnp.zeros((E, H), dtype=jnp.float32)
        W2 = jax.random.normal(ks[3], (E, H, D), dtype=jnp.float32) * 0.02
        b2 = jnp.zeros((E, D), dtype=jnp.float32)
        ln_gamma = jnp.ones((D,), dtype=jnp.float32)
        ln_beta = jnp.zeros((D,), dtype=jnp.float32)
        return {'x': x, 'gate_W': gate_W, 'gate_b': gate_b, 'W1': W1, 'b1': b1, 'W2': W2, 'b2': b2, 'ln_gamma': ln_gamma, 'ln_beta': ln_beta}
    _L0_ffn_all = _L0_ffn_setup()
    _L0_ffn_in = {k: v for k, v in _L0_ffn_all.items() if k in ('gate_W', 'gate_b', 'W1', 'b1', 'W2', 'b2', 'ln_gamma', 'ln_beta')}
    del _L0_ffn_all
    return {'x': x, 'ctx_1024': ctx_1024, 'L0_xattn_q_w': _L0_xattn_in['q_w'], 'L0_xattn_k_w': _L0_xattn_in['k_w'], 'L0_xattn_norm_w': _L0_xattn_in['norm_w'], 'L0_xattn_gate_w': _L0_xattn_in['gate_w'], 'L0_xattn_gate_b': _L0_xattn_in['gate_b'], 'L0_ffn_gate_W': _L0_ffn_in['gate_W'], 'L0_ffn_gate_b': _L0_ffn_in['gate_b'], 'L0_ffn_W1': _L0_ffn_in['W1'], 'L0_ffn_b1': _L0_ffn_in['b1'], 'L0_ffn_W2': _L0_ffn_in['W2'], 'L0_ffn_b2': _L0_ffn_in['b2'], 'L0_ffn_ln_gamma': _L0_ffn_in['ln_gamma'], 'L0_ffn_ln_beta': _L0_ffn_in['ln_beta']}

def reference(x, ctx_1024, L0_xattn_q_w, L0_xattn_k_w, L0_xattn_norm_w, L0_xattn_gate_w, L0_xattn_gate_b, L0_ffn_gate_W, L0_ffn_gate_b, L0_ffn_W1, L0_ffn_b1, L0_ffn_W2, L0_ffn_b2, L0_ffn_ln_gamma, L0_ffn_ln_beta):
    import jax
    import jax.numpy as jnp

    def _L0_xattn_ref(hidden_states, memory_state, q_w, k_w, norm_w, gate_w, gate_b):
        import jax, jax.numpy as jnp
        import numpy as np
        EPS = 1e-06

        def _rmsnorm(x, w, eps=EPS):
            x32 = x.astype(jnp.float32)
            var = jnp.mean(x32 * x32, axis=-1, keepdims=True)
            return (x32 * jax.lax.rsqrt(var + eps)).astype(x.dtype) * w
        B, S, H = hidden_states.shape
        K = memory_state.shape[1]
        scale = 1.0 / np.sqrt(H)
        normed = _rmsnorm(hidden_states, norm_w)
        v_pool = jnp.concatenate([normed, memory_state], axis=1)
        q = jnp.einsum('bsh,oh->bso', normed, q_w)
        k = jnp.einsum('bth,oh->bto', v_pool, k_w)
        logits = jnp.einsum('bsd,btd->bst', q, k) * scale
        local = jnp.tril(jnp.ones((S, S), bool))
        mask = jnp.concatenate([local, jnp.ones((S, K), bool)], axis=1)
        logits = jnp.where(mask[None], logits, -jnp.inf)
        attn = jax.nn.softmax(logits, axis=-1)
        h_tilde = jnp.einsum('bst,bth->bsh', attn, v_pool)
        alpha = jax.nn.sigmoid(jnp.einsum('bsh,oh->bso', hidden_states, gate_w) + gate_b)
        return (1.0 - alpha) * hidden_states + alpha * h_tilde

    def _L0_ffn_ref(x, gate_W, gate_b, W1, b1, W2, b2, ln_gamma, ln_beta):
        import jax, jax.numpy as jnp
        import numpy as np
        D = 128
        E = 8
        H = 256
        TOP_K = 2
        ALPHA = 0.5
        LN_EPS = 1e-05

        def _experts_all(x, W1, b1, W2, b2):
            h = jax.nn.relu(jnp.einsum('bld,edh->eblh', x, W1) + b1[:, None, None, :])
            return jnp.einsum('eblh,ehd->ebld', h, W2) + b2[:, None, None, :]

        def _selected_expert(x, expert_idx, W1, b1, W2, b2):
            oh = jax.nn.one_hot(expert_idx, E, dtype=x.dtype)
            return jnp.einsum('ebld,ble->bld', _experts_all(x, W1, b1, W2, b2), oh)

        def _layer_norm(x, gamma, beta):
            mu = jnp.mean(x, axis=-1, keepdims=True)
            var = jnp.mean(jnp.square(x - mu), axis=-1, keepdims=True)
            return (x - mu) * jax.lax.rsqrt(var + LN_EPS) * gamma + beta
        residual = x
        gate_logits = jnp.einsum('bld,de->ble', x, gate_W) + gate_b
        gate_weights = jax.nn.softmax(gate_logits, axis=-1)
        topk_vals, topk_idx = jax.lax.top_k(gate_weights, TOP_K)
        boost = jax.lax.stop_gradient(x)
        outs = []
        for i in range(TOP_K):
            eo = _selected_expert(boost, topk_idx[:, :, i], W1, b1, W2, b2)
            outs.append(eo)
            if i < TOP_K - 1:
                boost = boost + ALPHA * jax.lax.stop_gradient(eo)
        fused = sum((topk_vals[:, :, i:i + 1] * outs[i] for i in range(TOP_K)))
        return _layer_norm(residual + fused, ln_gamma, ln_beta)
    x = x + _L0_xattn_ref(_layernorm(x, axis=-1), ctx_1024, L0_xattn_q_w, L0_xattn_k_w, L0_xattn_norm_w, L0_xattn_gate_w, L0_xattn_gate_b)
    x = x + _L0_ffn_ref(_layernorm(x, axis=-1), L0_ffn_gate_W, L0_ffn_gate_b, L0_ffn_W1, L0_ffn_b1, L0_ffn_W2, L0_ffn_b2, L0_ffn_ln_gamma, L0_ffn_ln_beta)
    return x

_drawn_inputs = setup_inputs


def setup_inputs(seed=0):
    import zlib

    import numpy as np

    out = dict(_drawn_inputs(seed))
    spreads = {'L0_xattn_norm_w': (1.0, 0.6),
     'L0_xattn_gate_b': (0.0, 0.477),
     'L0_ffn_gate_b': (0.0, 0.8),
     'L0_ffn_b1': (0.0, 0.8),
     'L0_ffn_b2': (0.0, 0.8),
     'L0_ffn_ln_gamma': (1.0, 0.2),
     'L0_ffn_ln_beta': (0.0, 0.1)}
    factors = {'L0_ffn_gate_W': 6.209, 'L0_ffn_W1': 8.0, 'L0_ffn_W2': 8.0}
    for name, (base, spread) in spreads.items():
        noise = np.random.default_rng([zlib.crc32(name.encode()), seed]).standard_normal(out[name].shape)
        drawn = base * np.exp(spread * noise) if base else spread * noise
        out[name] = jnp.asarray(drawn.astype(out[name].dtype))
    for name, factor in factors.items():
        out[name] = (out[name] * factor).astype(out[name].dtype)
    return out
```

```python
from contextlib import ExitStack

import concourse.bass as bass
from concourse import mybir

F32 = mybir.dt.float32
BF16 = mybir.dt.bfloat16
U32 = mybir.dt.uint32
I32 = mybir.dt.int32
ALU = mybir.AluOpType
ACT = mybir.ActivationFunctionType
AX_X = mybir.AxisListType.X

B, S, D = 64, 128, 128
SC = 77
E, H = 8, 256
HH = H // 128
G = 2
NP = B // G
CODES = E * E
TILES = 120
T = S + SC
REC = 2 * D + 2
EPS_LN, EPS_RMS = 1e-5, 1e-6
NEG = -1.0e30
UNROLL = 4
TU = 8
SKIPPED = 1.0e6
WE = H + HH * D


def skewed(engine, count, unroll, lags, body):
    last = max(lags)
    first = -(-last // unroll) * unroll
    for i in range(first):
        body(i, i % unroll, [l for l in lags if i >= l])
    end = first + (count - first) // unroll * unroll
    with engine.Fori(first // unroll, end // unroll) as turn:
        for k in range(unroll):
            body(turn * unroll + k, k, lags)
    for i in range(end, count + last):
        body(i, i % unroll, [l for l in lags if 0 <= i - l < count])


def free(engine, semaphore, per, unit, depth):
    if isinstance(unit, int) and unit < depth:
        return
    engine.wait_ge(semaphore, (unit - (depth - 1)) * per)


def program(nc, x, ctx, q_w, k_w, norm_w, gate_w, gate_b, router_w, router_b, W1, b1, W2, b2,
            gamma, beta, out):
    stack = ExitStack()
    with stack:
        def sb(name, shape, dt=F32):
            return stack.enter_context(nc.sbuf_tensor(name, shape, dt))

        def sem(name):
            return stack.enter_context(nc.semaphore(name))

        out_rows = out.rearrange("b s d -> (b s) d")
        records = nc.dram_tensor("records", [B * S, REC], F32).ap()

        ident = sb("ident", [128, 128])
        ident_h = sb("ident_h", [128, 128], BF16)
        mask_h = sb("mask_h", [128, 128], BF16)
        before_h = sb("before_h", [128, 128], BF16)
        rest_h = sb("rest_h", [128, 128], BF16)
        ones_h = sb("ones_h", [128, 128], BF16)
        zeros_h = sb("zeros_h", [128, 128], BF16)
        codes_i = sb("codes_i", [128, 128], I32)
        codes_f = sb("codes_f", [128, 128])
        minus_half = sb("minus_half", [128, 2 * G])
        qw = sb("qw", [128, D])
        kw = sb("kw", [128, D])
        gw = sb("gw", [128, D])
        score_m = sb("score_m", [128, D])
        gwT = sb("gwT", [128, D])
        wcol = sb("wcol", [128, 1])
        w_bc = sb("w_bc", [128, G, D])
        beta_bc = sb("beta_bc", [128, G, D])
        gamma_bc = sb("gamma_bc", [128, D])
        rw = sb("rw", [128, E])
        rb_bc = sb("rb_bc", [128, G, E])
        We = sb("We", [128, E, WE])
        x_in = sb("x_in", [128, 4, G, D])
        c_in = sb("c_in", [SC, 4, G, D])
        stats = sb("stats", [128, G, 6])
        mv = sb("mv", [128, 2, G, 2])
        var_ab = sb("var_ab", [128, 2, 2, G])
        scale_ab = sb("scale_ab", [128, 2, 2, G])
        normed = sb("normed", [128, G, D])
        h0 = sb("h0", [128, 4, G, D])
        vw = sb("vw", [128, 2, G, D])
        xh = sb("xh", [128, 4, G, D])
        tT = sb("tT", [128, 2, 2, G, D])
        cA = sb("cA", [128, 2, G * SC + G * S])
        tanh_z = sb("tanh_z", [128, 4, G, D])
        negmax = sb("negmax", [128, 2, G])
        prob = sb("prob", [128, 2, G, T])
        denom = sb("denom", [128, 2, G])
        rden = sb("rden", [128, G])
        pTs = sb("pTs", [128, 2, G, S])
        pTc = sb("pTc", [SC, 2, G, S])
        diff = sb("diff", [128, G, D])
        gated = sb("gated", [128, G, D])
        x1 = sb("x1", [128, 2, G, D])
        stats1 = sb("stats1", [128, G, 6])
        mv1 = sb("mv1", [128, 2, G, 2])
        var1 = sb("var1", [128, 2, G])
        scale1 = sb("scale1", [128, 2, G])
        rec = sb("rec", [128, 2, G, REC])
        h1T = sb("h1T", [128, 2, G, S])
        lg = sb("lg", [128, G, E])
        top = sb("top", [128, G, E])
        topi = sb("topi", [128, G, E], U32)
        ldiff = sb("ldiff", [128, 2, G, E])
        lexp = sb("lexp", [128, 2, G, E])
        lsum = sb("lsum", [128, G])
        code = sb("code", [128, 64])
        hot = sb("hot", [128, 64, CODES], BF16)
        hotR = sb("hotR", [128, G, CODES])
        rank = sb("rank", [128, 64])

        bias_col = sb("bias_col", [128, 25])
        part0 = sb("part0", [128, 3, 25], BF16)
        rest1 = sb("rest1", [128, 25])
        rest2 = sb("rest2", [128, 25])
        b1s = sb("b1s", [3, E, H], BF16)
        b2s = sb("b2s", [3, E, D], BF16)
        gbs = sb("gbs", [3, D], BF16)
        count_i = sb("count_i", [128, CODES], I32)
        tiles_i = sb("tiles_i", [128, CODES], I32)
        tiles_f = sb("tiles_f", [128, CODES])
        tile_end = sb("tile_end", [128, CODES])
        ones_f = sb("ones_f", [128, CODES])
        start_h = sb("start_h", [128, CODES], BF16)
        hot_start = sb("hot_start", [128, 64, CODES], BF16)
        start_of = sb("start_of", [128, 64])
        rank_i = sb("rank_i", [128, 64], I32)
        rank_hi = sb("rank_hi", [128, 64], I32)
        rank_lo = sb("rank_lo", [128, 64], I32)
        tile_of = sb("tile_of", [128, 64])
        place = sb("place", [128, 64])
        token_i = sb("token_i", [128, 64], I32)
        token_f = sb("token_f", [128, 64])
        part_i = sb("part_i", [128, 1], I32)
        part_f = sb("part_f", [128, 1])
        is_place = sb("is_place", [128, 4, 128])
        is_tile = sb("is_tile", [128, 4, TILES])
        ended = sb("ended", [128, CODES])
        tile_code = sb("tile_code", [128, 1])
        tile_row = sb("tile_row", [1, 128], I32)
        expert_row = sb("expert_row", [1, 2, 128], I32)
        slots = sb("slots", [128, TILES])
        empty = sb("empty", [128, TILES])
        gather_at = sb("gather_at", [128, TILES], U32)
        scatter_at = sb("scatter_at", [128, TILES], U32)
        gather_now = sb("gather_now", [128, TU], U32)
        scatter_now = sb("scatter_now", [128, TU], U32)
        tok = sb("tok", [128, TU, REC])
        h1t = sb("h1t", [128, 2, 128])
        hid1 = sb("hid1", [128, 2, H])
        hid1t = sb("hid1t", [128, 2, HH, 128])
        boost = sb("boost", [128, 2, D])
        mixed = sb("mixed", [128, 4, D])
        boostt = sb("boostt", [128, 2, 128])
        hid2 = sb("hid2", [128, 2, H])
        hid2t = sb("hid2t", [128, 2, HH, 128])
        z = sb("z", [128, 2, D])
        statsz = sb("statsz", [128, 6])
        mvz = sb("mvz", [128, 2, 2])
        varz = sb("varz", [128, 2])
        scalez = sb("scalez", [128, 2])
        y = sb("y", [128, D])
        row_out = sb("row_out", [128, 4, D])

        def bank(name):
            return stack.enter_context(nc.psum_tensor(name, [128, 512], F32))

        bT, bC, bL, bP, bZ, bO, bH, bR = [bank(f"bank{n}") for n in range(8)]

        s_w = sem("weights_in")
        s_we = sem("experts_in")
        s_c = sem("constants")
        s_setup_pe = sem("setup_pe")
        s_setup_act = sem("setup_act")
        x_ready = [sem(f"x_ready{k}") for k in range(4)]
        D1 = sem("stats_ready")
        P1 = sem("scales_ready")
        D2 = sem("h0_ready")
        P2 = sem("vw_ready")
        P2h = sem("xh_ready")
        T1 = sem("tokens_transposed")
        A1 = sem("tT_ready")
        M1 = sem("scoremix_done")
        A2 = sem("cA_ready")
        A2z = sem("tanh_ready")
        M1z = sem("gate_done")
        M2 = sem("scores_done")
        D3 = sem("max_ready")
        A3 = sem("prob_ready")
        T2 = sem("prob_transposed")
        A4 = sem("pT_ready")
        M3 = sem("attended")
        D4 = sem("x1_ready")
        D4o = sem("attended_used")
        D5 = sem("stats1_ready")
        P3 = sem("scale1_ready")
        D6 = sem("h1_ready")
        P4 = sem("x1b_ready")
        T3 = sem("h1_transposed")
        A5 = sem("h1T_ready")
        M4 = sem("router_done")
        D7 = sem("hot_ready")
        D7l = sem("router_used")
        D7d = sem("top_ready")
        A6 = sem("lexp_ready")
        M5 = sem("rank_done")
        D8 = sem("rank_used")
        V_rank = sem("v_rank")
        D9 = sem("weights_ready")
        M6 = sem("rank_base_done")
        s_rec = [sem(f"records_out{b}") for b in range(2)]
        V_stats, V_mv = sem("v_stats"), sem("v_mv")
        V_stats1, V_mv1 = sem("v_stats1"), sem("v_mv1")
        V_rden, V_diff, V_gated = sem("v_rden"), sem("v_diff"), sem("v_gated")
        V_top, V_topi, V_code = sem("v_top"), sem("v_topi"), sem("v_code")
        V_lsum, V_v1 = sem("v_lsum"), sem("v_v1")

        V_part = sem("v_part")
        vs = sem("v_setup")
        s_bout, s_bin = sem("bias_parts_out"), sem("bias_parts_in")
        vb = sem("v_sorting")
        B_place, B_free, B_done = sem("place_ready"), sem("place_used"), sem("slots_done")
        B_col, B_row, B_rowdone = sem("tile_code_ready"), sem("tile_row_done"), sem("expert_row_ready")
        B_idx = sem("indices_ready")
        X_gather, X_scatter = sem("gather_now_ready"), sem("scatter_now_ready")
        g_in = [sem(f"gathered{k}") for k in range(TU)]
        g_out = [sem(f"scattered{k}") for k in range(4)]
        C1, C1e = sem("c_h1_transposed"), sem("c_h1t_ready")
        C2, C2e = sem("c_hidden1_done"), sem("c_hid1_ready")
        C3, C3e = sem("c_hid1_transposed"), sem("c_hid1t_ready")
        C4, C4b, C4e = sem("c_out1_done"), sem("c_boost_ready"), sem("c_mixed_ready")
        C5, C5e = sem("c_boost_transposed"), sem("c_boostt_ready")
        C6, C6e = sem("c_hidden2_done"), sem("c_hid2_ready")
        C7, C7e = sem("c_hid2_transposed"), sem("c_hid2t_ready")
        C8, C8e = sem("c_out2_done"), sem("c_z_ready")
        V_zs, V_zm, C9 = sem("v_zstats"), sem("v_zmv"), sem("c_var_ready")
        C10, V_y, C11 = sem("c_scale_ready"), sem("v_y"), sem("c_row_ready")

        block = stack.enter_context(nc.Block())

        x_v = x.rearrange("(n g) s d -> n s g d", g=G)
        c_v = ctx.rearrange("(n g) s d -> n s g d", g=G)
        rec_v = records.rearrange("(n g s) r -> n s g r", g=G, s=S)
        SETUP_LOADS = 5 + 3 * G + 1 + 3
        parts = nc.dram_tensor("bias_parts", [3, 128 * 25], BF16).ap()
        BIAS = ((0, E * H // 128), (E * H // 128, E * D // 128), (24, 1))

        @block.sync
        def _(sp):
            def load(i, k):
                if not (isinstance(i, int) and i < 4):
                    sp.wait_ge(P2h, i - 3)
                    sp.wait_ge(M3, i - 3)
                sp.dma_start(x_in[:, k, :, :], x_v[i]).then_inc(x_ready[k], 16)
                sp.dma_start(c_in[:, k, :, :], c_v[i]).then_inc(x_ready[k], 16)

            load(0, 0)
            for dst, src in ((qw, q_w), (kw, k_w), (gw, gate_w), (rw, router_w)):
                sp.dma_start(dst[:, :], src).then_inc(s_w, 16)
            sp.dma_start(wcol[:, :], norm_w.rearrange("(p a) -> p a", a=1)).then_inc(s_w, 16)
            for (at, n), src in zip(BIAS, (b1.rearrange("e (a f) -> (e a) f", f=16), b2.rearrange("e (a f) -> (e a) f", f=8),
                                          gate_b.rearrange("(p a) -> p a", a=1))):
                sp.dma_start(bias_col[:, at:at + n], src).then_inc(s_w, 16)
            load(1, 1)
            row = lambda v: v.rearrange("(a n) -> a n", a=1).to_broadcast([128, v.shape[0]])
            for g in range(G):
                sp.dma_start(w_bc[:, g, :], row(norm_w)).then_inc(s_w, 16)
                sp.dma_start(rb_bc[:, g, :], row(router_b)).then_inc(s_w, 16)
                sp.dma_start(beta_bc[:, g, :], row(beta)).then_inc(s_w, 16)
            sp.dma_start(gamma_bc[:, :], row(gamma)).then_inc(s_w, 16)
            sp.wait_ge(V_part, 1)
            for at, n in BIAS:
                sp.dma_start(parts[:, 128 * at:128 * (at + n)].rearrange("t (p f) -> p t f", f=n),
                             part0[:, :, at:at + n], allow_slow_non_contiguous=n == 1).then_inc(s_bout, 16)
            sp.wait_ge(s_bout, 48)
            for (at, n), dst in zip(BIAS, (b1s[:, :, :].rearrange("t e h -> t (e h)"),
                                           b2s[:, :, :].rearrange("t e d -> t (e d)"), gbs[:, :])):
                sp.dma_start(dst, parts[:, 128 * at:128 * (at + n)]).then_inc(s_bin, 16)

            def body(i, k, live):
                if 0 in live and not (isinstance(i, int) and i < 2):
                    load(i, k)
                if 5 in live:
                    q = i - 5
                    b = (k - 5) % 2
                    sp.wait_ge(D6, q + 1)
                    sp.wait_ge(P4, q + 1)
                    sp.wait_ge(D9, q + 1)
                    sp.dma_start(rec_v[q], rec[:, b, :, :]).then_inc(s_rec[b], 16)
            skewed(sp, NP, UNROLL, [0, 5], body)
            for b in range(2):
                sp.wait_ge(s_rec[b], 8 * NP)

        @block.gpsimd
        def _(pool):
            pool.memset(ident[:, :], 0.0)
            pool.memset(ident_h[:, :], 0.0)
            pool.memset(mask_h[:, :], 0.0)
            pool.memset(before_h[:, :], 0.0)
            pool.memset(rest_h[:, :], 0.0)
            pool.memset(ones_h[:, :], 1.0)
            pool.memset(zeros_h[:, :], 0.0)
            pool.memset(minus_half[:, :], -0.5)
            pool.iota(codes_i[:, :], [[1, 128]], base=0, channel_multiplier=0).then_inc(s_c, 1)
            pool.wait_ge(s_c, 1)
            for m in (ident, ident_h):
                pool.affine_select(out=m[:, :], in_=m[:, :], compare_op=ALU.not_equal, fill=1.0, base=0,
                                   pattern=[[-1, 128]], channel_multiplier=1)
            pool.affine_select(out=mask_h[:, :], in_=mask_h[:, :], compare_op=ALU.is_ge, fill=NEG, base=0,
                               pattern=[[-1, 128]], channel_multiplier=1)
            pool.affine_select(out=before_h[:, :], in_=before_h[:, :], compare_op=ALU.is_ge, fill=1.0, base=0,
                               pattern=[[-1, 128]], channel_multiplier=1)
            pool.affine_select(out=rest_h[:, :], in_=rest_h[:, :], compare_op=ALU.is_gt, fill=1.0, base=0,
                               pattern=[[1, 128]], channel_multiplier=-1)
            pool.tensor_copy(codes_f[:, :], codes_i[:, :]).then_inc(s_c, 1)
            pool.iota(token_i[:, :], [[S, B]], base=1, channel_multiplier=1)
            pool.iota(part_i[:, :], [[0, 1]], base=0, channel_multiplier=1)
            pool.memset(ones_f[:, :], 1.0).then_inc(s_c, 1)

            def body(i, k, live):
                if 1 in live:
                    q, r, b = i - 1, (k - 1) % 4, (k - 1) % 2
                    if isinstance(q, int) and q == 0:
                        pool.wait_ge(s_w, 16 * SETUP_LOADS)
                    pool.wait_ge(D2, q + 1)
                    free(pool, M3, 1, q, 2)
                    pool.tensor_tensor(vw[:, b, :, :], normed[:, :, :], w_bc[:, :, :], ALU.mult).then_inc(P2, 1)
                    free(pool, D4, 1, q, 4)
                    pool.tensor_tensor(xh[:, r, :, :], x_in[:, r, :, :], h0[:, r, :, :], ALU.add).then_inc(P2h, 1)
                if 0 in live:
                    q, b = i, k % 2
                    pool.wait_ge(D1, q + 1)
                    free(pool, D2, 1, q, 2)
                    pool.tensor_tensor(scale_ab[:, b].rearrange("p a g -> p (a g)"),
                                       var_ab[:, b].rearrange("p a g -> p (a g)"),
                                       minus_half[:, :], ALU.pow).then_inc(P1, 1)
                if 3 in live:
                    q, b = i - 3, (k - 3) % 2
                    pool.wait_ge(D5, q + 1)
                    free(pool, D6, 1, q, 2)
                    pool.tensor_tensor(scale1[:, b, :], var1[:, b, :], minus_half[:, 0:G], ALU.pow).then_inc(P3, 1)
                if 3 in live:
                    q, b = i - 3, (k - 3) % 2
                    pool.wait_ge(D4, q + 1)
                    if not (isinstance(q, int) and q < 2):
                        pool.wait_ge(s_rec[b], (q - b) * 8)
                    pool.tensor_tensor(rec[:, b, :, D:2 * D], x1[:, b, :, :], beta_bc[:, :, :], ALU.add).then_inc(P4, 1)
            skewed(pool, NP, UNROLL, [0, 1, 2, 3], body)

            pool.wait_ge(B_idx, 1)
            for b in range(2):
                pool.wait_ge(s_rec[b], 8 * NP)

            def tile(i, k, live):
                if 0 in live:
                    t = i
                    if k % 4 == 0:
                        if not (isinstance(t, int) and t < TU):
                            pool.wait_ge(C1, t - 4)
                        pool.tensor_copy(gather_now[:, k:k + 4], gather_at[:, bass.ds(t, 4)]).then_inc(X_gather, 4)
                        pool.wait_ge(X_gather, t + 4)
                    if not (isinstance(t, int) and t < TU):
                        pool.wait_ge(C11, t - (TU - 1))
                        pool.nop(nofuse=True)
                    pool.indirect_dma_start(tok[:, k, :], None, records,
                                            bass.IndirectOffsetOnAxis(ap=gather_now[:, k:k + 1], axis=0)
                                            ).then_inc(g_in[k], 16)
                if 6 in live:
                    t, b = i - 6, k % 2
                    pool.wait_ge(C9, t + 1)
                    pool.tensor_tensor(scalez[:, b:b + 1], varz[:, b:b + 1], minus_half[:, 0:1], ALU.pow).then_inc(C10, 1)
                if 7 in live:
                    t, r, n = i - 7, (k - 7) % 4, (k - 7) % TU
                    if n % 4 == 0:
                        if not (isinstance(t, int) and t < TU):
                            pool.wait_ge(C11, t)
                        pool.tensor_copy(scatter_now[:, n:n + 4], scatter_at[:, bass.ds(t, 4)]).then_inc(X_scatter, 4)
                        pool.wait_ge(X_scatter, t + 4)
                    pool.wait_ge(C11, t + 1)
                    pool.nop(nofuse=True)
                    pool.indirect_dma_start(out_rows, bass.IndirectOffsetOnAxis(ap=scatter_now[:, n:n + 1], axis=0),
                                            row_out[:, r, :], None, bounds_check=B * S - 1, oob_is_err=False
                                            ).then_inc(g_out[r], 16)
            skewed(pool, TILES, TU, [0, 6, 7], tile)
            for r in range(4):
                pool.wait_ge(g_out[r], 16 * (TILES // 4))

        @block.tensor
        def _(pe):
            pe.wait_ge(s_c, 2)
            pe.matmul(bR[:, 0:G * CODES], ones_h[:, :], zeros_h[:, :], start=True, stop=False, skip_group_check=True)
            pe.wait_ge(s_w, 16 * SETUP_LOADS)
            pe.matmul(bL[:, 0:128], qw[:, :], kw[:, :], start=True, stop=True)
            pe.transpose(bL[:, 128:256], gw[:, :], ident[:, :]).then_inc(s_setup_pe, 1)

            def body(i, k, live):
                first = isinstance(i, int)
                if 4 in live:
                    q, b = i - 4, k % 2
                    pe.wait_ge(A5, q + 1)
                    for g in range(G):
                        mm = pe.matmul(bH[:, G * S + g * E:G * S + (g + 1) * E], h1T[:, b, g, :], rw[:, :],
                                       start=True, stop=True)
                    mm.then_inc(M4, 1)
                if 1 in live:
                    q, r, b = i - 1, (k - 1) % 4, (k - 1) % 2
                    pe.wait_ge(x_ready[r], (q - r) * 8 + 32)
                    free(pe, A2, 1, q, 1)
                    for g in range(G):
                        pe.transpose(bC[:, g * SC:(g + 1) * SC], c_in[:, r, g, :], ident[0:SC, 0:SC])
                    pe.wait_ge(D2, q + 1)
                    free(pe, A1, 1, q, 1)
                    for g in range(G):
                        pe.transpose(bT[:, (G + g) * S:(G + g + 1) * S], h0[:, r, g, :], ident[:, :])
                    pe.wait_ge(P2, q + 1)
                    for g in range(G):
                        mm = pe.transpose(bT[:, g * S:(g + 1) * S], vw[:, b, g, :], ident[:, :])
                    mm.then_inc(T1, 1)
                if 2 in live:
                    q, b = i - 2, (k - 2) % 2
                    pe.wait_ge(A3, q + 1)
                    free(pe, A4, 1, q, 1)
                    for g in range(G):
                        pe.transpose(bP[:, g * S:(g + 1) * S], prob[:, b, g, 0:S], ident[:, :])
                        mm = pe.transpose(bP[0:SC, (G + g) * S:(G + g + 1) * S], prob[:, b, g, S:T], ident[:, :])
                    mm.then_inc(T2, 1)
                if 1 in live:
                    q, b = i - 1, (k - 1) % 2
                    if first and q == 0:
                        pe.wait_ge(s_setup_act, 1)
                    pe.wait_ge(A1, q + 1)
                    pe.matmul(bC[:, G * SC:G * SC + G * S], score_m[:, :],
                              tT[:, b, 0, :, :].rearrange("p g s -> p (g s)"), start=True, stop=True).then_inc(M1, 1)
                    free(pe, A2z, 1, q, 1)
                    if first and q == 0:
                        pe.wait_ge(s_bin, 48)
                    for g in range(G):
                        pe.matmul(bZ[:, g * D:(g + 1) * D], tT[:, b, 1, g, :], gwT[:, :], start=True, stop=False)
                        mm = pe.matmul(bZ[:, g * D:(g + 1) * D], ones_h[0:3, :], gbs[:, :], start=False, stop=True)
                    mm.then_inc(M1z, 1)
                if 2 in live:
                    q, r, b = i - 2, (k - 2) % 4, (k - 2) % 2
                    pe.wait_ge(A4, q + 1)
                    free(pe, D4o, 1, q, 1)
                    for g in range(G):
                        pe.matmul(bO[:, g * D:(g + 1) * D], pTs[:, b, g, :], vw[:, b, g, :], start=True, stop=False)
                        mm = pe.matmul(bO[:, g * D:(g + 1) * D], pTc[:, b, g, :], c_in[:, r, g, :], start=False, stop=True)
                    mm.then_inc(M3, 1)
                if 4 in live:
                    q = i - 4
                    pe.wait_ge(D7, q + 1)
                    pair_hot = hot[:, bass.ts(q, G), :].rearrange("p g c -> p (g c)")
                    pe.matmul(bR[:, 0:G * CODES], before_h[:, :], pair_hot, start=False,
                              stop=False, skip_group_check=True)
                    pe.matmul(bR[:, CODES:2 * CODES], ones_h[:, :], pair_hot[:, 0:CODES], start=False, stop=False,
                              skip_group_check=True).then_inc(M5, 1)
                if 1 in live:
                    q, b = i - 1, (k - 1) % 2
                    pe.wait_ge(A2, q + 1)
                    free(pe, A3, 1, q, 1)
                    for g in range(G):
                        A = cA[:, b, G * SC + g * S:G * SC + (g + 1) * S]
                        o = g * 256
                        pe.matmul(bL[:, o:o + S], A, tT[:, b, 0, g, :], start=True, stop=False)
                        pe.matmul(bL[:, o:o + S], ident_h[:, :], mask_h[:, :], start=False, stop=True)
                        mm = pe.matmul(bL[:, o + S:o + T], A, cA[:, b, g * SC:(g + 1) * SC], start=True, stop=True)
                    mm.then_inc(M2, 1)
                if 4 in live:
                    q = i - 4
                    pe.wait_ge(D8, q + 1)
                    pair_hot = hot[:, bass.ts(q, G), :].rearrange("p g c -> p (g c)")
                    pe.matmul(bR[:, 0:G * CODES], rest_h[:, :], pair_hot, start=False, stop=False,
                              skip_group_check=True)
                    pe.matmul(bR[:, 0:CODES], ones_h[:, :], pair_hot[:, CODES:2 * CODES], start=False, stop=False,
                              skip_group_check=True).then_inc(M6, 1)
                if 3 in live:
                    q, b = i - 3, (k - 3) % 2
                    pe.wait_ge(D6, q + 1)
                    free(pe, D7l, 1, q, 1)
                    for g in range(G):
                        mm = pe.transpose(bH[:, g * S:(g + 1) * S], rec[:, b, g, 0:D], ident[:, :])
                    mm.then_inc(T3, 1)
            skewed(pe, NP, UNROLL, [0, 1, 2, 3, 4], body)

            pe.wait_ge(D4o, NP)

            def batch(i, k, live):
                pe.wait_ge(B_place, i + 1)
                pe.matmul(bO[:, 0:TILES], is_place[:, k, :], is_tile[:, k, :],
                          start=isinstance(i, int) and i == 0, stop=isinstance(i, int) and i == B - 1,
                          skip_group_check=True).then_inc(B_free, 1)
            for i in range(4):
                batch(i, i, None)
            with pe.Fori(1, B // 4 - 1) as turn:
                for k in range(4):
                    batch(turn * 4 + k, k, None)
            for i in range(B - 4, B):
                batch(i, i % 4, None)
            pe.wait_ge(B_col, 1)
            pe.matmul(bP[0:1, 0:128], tile_code[:, :], ident[:, :], start=True, stop=True).then_inc(B_row, 1)

            pe.wait_ge(s_we, 16 * 2 * E)
            pe.wait_ge(B_rowdone, 1)

            def expert(which, t):
                return pe.value_load(expert_row[0:1, which, bass.ds(t, 1)], min_val=0, max_val=E - 1)

            def up(dst, lhsT, e):
                pe.matmul(dst, lhsT, We[:, bass.ds(e, 1), 0:H], start=True, stop=False)
                return pe.matmul(dst, ones_h[0:3, :], b1s[:, bass.ds(e, 1), :], start=False, stop=True)

            def down(dst, hT, e):
                for s in range(HH):
                    pe.matmul(dst, hT[:, s, :], We[:, bass.ds(e, 1), H + s * D:H + (s + 1) * D], start=s == 0, stop=False)
                return pe.matmul(dst, ones_h[0:3, :], b2s[:, bass.ds(e, 1), :], start=False, stop=True)

            def tile(i, k, live):
                if 2 in live:
                    t, r = i - 2, (k - 2) % TU
                    pe.wait_ge(g_in[r], (t - r) * 2 + 16)
                    free(pe, C1e, 1, t, 1)
                    pe.transpose(bT[:, 0:128], tok[:, r, 0:D], ident[:, :]).then_inc(C1, 1)
                if 3 in live:
                    t, b = i - 3, (k - 3) % 2
                    pe.wait_ge(C2e, t + 1)
                    free(pe, C3e, 1, t, 1)
                    for s in range(HH):
                        mm = pe.transpose(bL[:, s * 128:(s + 1) * 128], hid1[:, b, s * 128:(s + 1) * 128], ident[:, :])
                    mm.then_inc(C3, 1)
                if 5 in live:
                    t, b = i - 5, (k - 5) % 2
                    e = expert(1, t)
                    pe.wait_ge(C5e, t + 1)
                    free(pe, C6e, 1, t, 1)
                    up(bO[:, 0:H], boostt[:, b, :], e).then_inc(C6, 1)
                if 4 in live:
                    t, b = i - 4, k % 2
                    pe.wait_ge(C4b, t + 1)
                    free(pe, C5e, 1, t, 1)
                    pe.transpose(bZ[:, 0:128], boost[:, b, :], ident[:, :]).then_inc(C5, 1)
                if 6 in live:
                    t, b = i - 6, k % 2
                    e = expert(1, t)
                    pe.wait_ge(C7e, t + 1)
                    free(pe, C8e, 1, t, 1)
                    down(bR[:, 0:D], hid2t[:, b], e).then_inc(C8, 1)
                if 2 in live:
                    t, b = i - 2, k % 2
                    e = expert(0, t)
                    pe.wait_ge(C1e, t + 1)
                    free(pe, C2e, 1, t, 1)
                    up(bC[:, 0:H], h1t[:, b, :], e).then_inc(C2, 1)
                if 5 in live:
                    t, b = i - 5, (k - 5) % 2
                    pe.wait_ge(C6e, t + 1)
                    free(pe, C7e, 1, t, 1)
                    for s in range(HH):
                        mm = pe.transpose(bH[:, s * 128:(s + 1) * 128], hid2[:, b, s * 128:(s + 1) * 128], ident[:, :])
                    mm.then_inc(C7, 1)
                if 3 in live:
                    t, b = i - 3, (k - 3) % 2
                    e = expert(0, t)
                    pe.wait_ge(C3e, t + 1)
                    free(pe, C4e, 1, t, 1)
                    down(bP[:, 0:D], hid1t[:, b], e).then_inc(C4, 1)
            skewed(pe, TILES, TU, [2, 3, 4, 5, 6], tile)

        @block.scalar
        def _(act):
            for e in range(E):
                act.dma_start(We[:, e, 0:H], W1[e]).then_inc(s_we, 16)
                act.dma_start(We[:, e, H:WE].rearrange("p (s d) -> p s d", s=HH),
                              W2[e].rearrange("(s p) d -> p s d", p=128)).then_inc(s_we, 16)
            act.wait_ge(s_setup_pe, 1)
            act.activation(score_m[:, :], bL[:, 0:128], ACT.Copy, scale=D ** -0.5)
            act.activation(gwT[:, :], bL[:, 128:256], ACT.Copy).then_inc(s_setup_act, 1)

            def body(i, k, live):
                if 2 in live:
                    q, b = i - 2, (k - 2) % 2
                    act.wait_ge(D3, q + 1)
                    free(act, T2, 1, q, 2)
                    for g in range(G):
                        a = act.activation(prob[:, b, g, :], bL[:, g * 256:g * 256 + T], ACT.Exp,
                                           bias=negmax[:, b, g:g + 1], accum_out=denom[:, b, g:g + 1])
                    a.then_inc(A3, 1)
                if 1 in live:
                    q, b = i - 1, (k - 1) % 2
                    act.wait_ge(T1, q + 1)
                    free(act, M2, 1, q, 2)
                    act.activation(tT[:, b].rearrange("p a g s -> p (a g s)"), bT[:, :], ACT.Copy).then_inc(A1, 1)
                if 2 in live:
                    q, b = i - 2, (k - 2) % 2
                    act.wait_ge(T2, q + 1)
                    free(act, M3, 1, q, 2)
                    act.activation(pTs[:, b].rearrange("p g s -> p (g s)"), bP[:, 0:G * S], ACT.Copy)
                    act.activation(pTc[:, b].rearrange("p g s -> p (g s)"), bP[0:SC, G * S:2 * G * S],
                                   ACT.Copy).then_inc(A4, 1)
                if 1 in live:
                    q, r, b = i - 1, (k - 1) % 4, (k - 1) % 2
                    act.wait_ge(M1, q + 1)
                    act.activation(cA[:, b, :], bC[:, 0:G * SC + G * S], ACT.Copy).then_inc(A2, 1)
                    act.wait_ge(M1z, q + 1)
                    free(act, D4, 1, q, 4)
                    act.activation(tanh_z[:, r].rearrange("p g d -> p (g d)"), bZ[:, 0:G * D], ACT.Tanh,
                                   scale=0.5).then_inc(A2z, 1)
                if 4 in live:
                    q, b = i - 4, k % 2
                    act.wait_ge(D7d, q + 1)
                    act.activation(lexp[:, b].rearrange("p g e -> p (g e)"), ldiff[:, b].rearrange("p g e -> p (g e)"),
                                   ACT.Exp).then_inc(A6, 1)
                if 3 in live:
                    q, b = i - 3, (k - 3) % 2
                    act.wait_ge(T3, q + 1)
                    free(act, M4, 1, q, 2)
                    act.activation(h1T[:, b].rearrange("p g s -> p (g s)"), bH[:, 0:G * S], ACT.Copy).then_inc(A5, 1)
            skewed(act, NP, UNROLL, [0, 1, 2, 3, 4], body)

            def tile(i, k, live):
                if 2 in live:
                    t, b = i - 2, k % 2
                    act.wait_ge(C1, t + 1)
                    free(act, C2, 1, t, 2)
                    act.activation(h1t[:, b, :], bT[:, 0:128], ACT.Copy).then_inc(C1e, 1)
                if 5 in live:
                    t, b = i - 5, (k - 5) % 2
                    act.wait_ge(C6, t + 1)
                    free(act, C7, 1, t, 2)
                    act.activation(hid2[:, b, :], bO[:, 0:H], ACT.Relu).then_inc(C6e, 1)
                if 4 in live:
                    t, b = i - 4, k % 2
                    act.wait_ge(C5, t + 1)
                    free(act, C6, 1, t, 2)
                    act.activation(boostt[:, b, :], bZ[:, 0:128], ACT.Copy).then_inc(C5e, 1)
                if 2 in live:
                    t, b = i - 2, k % 2
                    act.wait_ge(C2, t + 1)
                    free(act, C3, 1, t, 2)
                    act.activation(hid1[:, b, :], bC[:, 0:H], ACT.Relu).then_inc(C2e, 1)
            skewed(act, TILES, TU, [2, 4, 5], tile)

        @block.vector
        def _(dve):
            def body(i, k, live):
                first = isinstance(i, int)
                if 1 in live:
                    q, r, b = i - 1, (k - 1) % 4, (k - 1) % 2
                    dve.wait_ge(P1, q + 1)
                    free(dve, P2, 1, q, 1)
                    for g in range(G):
                        dve.tensor_scalar(normed[:, g, :], x_in[:, r, g, :], mv[:, b, g, 0:1], scale_ab[:, b, 0, g:g + 1],
                                          ALU.subtract, ALU.mult)
                        v = dve.tensor_scalar(h0[:, r, g, :], x_in[:, r, g, :], mv[:, b, g, 0:1], scale_ab[:, b, 1, g:g + 1],
                                              ALU.subtract, ALU.mult)
                    v.then_inc(D2, 1)
                if 2 in live:
                    q, b = i - 2, (k - 2) % 2
                    dve.wait_ge(M2, q + 1)
                    dve.tensor_reduce(negmax[:, b, :], bL[:, :].rearrange("p (g t) -> p g t", g=G)[:, :, 0:T],
                                      AX_X, ALU.max, negate=True).then_inc(D3, 1)
                if 0 in live:
                    q, r, b = i, k, k % 2
                    dve.wait_ge(x_ready[r], (q - r) * 8 + 32)
                    for g in range(G):
                        v = dve.bn_stats(stats[:, g, :], x_in[:, r, g, :])
                    v.then_inc(V_stats, 1)
                    dve.wait_ge(V_stats, q + 1)
                    dve.nop(nofuse=True)
                    for g in range(G):
                        v = dve.bn_aggr(mv[:, b, g, :], stats[:, g, :])
                    v.then_inc(V_mv, 1)
                    dve.wait_ge(V_mv, q + 1)
                    dve.tensor_scalar(var_ab[:, b, 0, :], mv[:, b, :, 1], 1.0 + EPS_RMS, EPS_RMS * EPS_LN,
                                      ALU.mult, ALU.add)
                    dve.tensor_scalar(var_ab[:, b, 1, :], mv[:, b, :, 1], EPS_LN, None, ALU.add).then_inc(D1, 1)
                if 4 in live:
                    q, b = i - 4, k % 2
                    dve.wait_ge(M4, q + 1)
                    dve.tensor_tensor(lg[:, :, :], bH[:, G * S:G * S + G * E].rearrange("p (g e) -> p g e", g=G),
                                      rb_bc[:, :, :], ALU.add).then_inc(D7l, 1)
                if 3 in live:
                    q, r, b = i - 3, (k - 3) % 4, (k - 3) % 2
                    dve.wait_ge(M3, q + 1)
                    dve.reciprocal(rden[:, :], denom[:, b, :]).then_inc(V_rden, 1)
                    dve.wait_ge(V_rden, q + 1)
                    for g in range(G):
                        v = dve.scalar_tensor_tensor(diff[:, g, :], bO[:, g * D:(g + 1) * D], rden[:, g:g + 1],
                                                     h0[:, r, g, :], ALU.mult, ALU.subtract)
                    v.then_inc(D4o, 1)
                    dve.wait_ge(D4o, q + 1)
                    dve.wait_ge(A2z, q + 1)
                    dve.scalar_tensor_tensor(gated[:, :, :], tanh_z[:, r, :, :], 1.0, diff[:, :, :],
                                             ALU.add, ALU.mult).then_inc(V_gated, 1)
                    dve.wait_ge(V_gated, q + 1)
                    dve.wait_ge(P2h, q + 1)
                    free(dve, P4, 1, q, 2)
                    dve.scalar_tensor_tensor(x1[:, b, :, :], gated[:, :, :], 0.5, xh[:, r, :, :],
                                             ALU.mult, ALU.add).then_inc(D4, 1)
                    dve.wait_ge(D4, q + 1)
                    for g in range(G):
                        v = dve.bn_stats(stats1[:, g, :], x1[:, b, g, :])
                    v.then_inc(V_stats1, 1)
                    dve.wait_ge(V_stats1, q + 1)
                    dve.nop(nofuse=True)
                    for g in range(G):
                        v = dve.bn_aggr(mv1[:, b, g, :], stats1[:, g, :])
                    v.then_inc(V_mv1, 1)
                    dve.wait_ge(V_mv1, q + 1)
                    dve.tensor_scalar(var1[:, b, :], mv1[:, b, :, 1], EPS_LN, None, ALU.add).then_inc(D5, 1)
                if 4 in live:
                    q, b = i - 4, k % 2
                    dve.wait_ge(D7l, q + 1)
                    dve.nop(nofuse=True)
                    for g in range(G):
                        v = dve.max(top[:, g, :], lg[:, g, :])
                    v.then_inc(V_top, 1)
                    dve.wait_ge(V_top, q + 1)
                    dve.nop(nofuse=True)
                    for g in range(G):
                        v = dve.max_index(topi[:, g, :], top[:, g, :], lg[:, g, :])
                    v.then_inc(V_topi, 1)
                    dve.tensor_tensor(ldiff[:, b, :, :], top[:, :, :], top[:, :, 0:1].to_broadcast([128, G, E]),
                                      ALU.subtract).then_inc(D7d, 1)
                    dve.wait_ge(V_topi, q + 1)
                    dve.scalar_tensor_tensor(code[:, bass.ts(q, G)], topi[:, :, 0], float(E), topi[:, :, 1],
                                             ALU.mult, ALU.add).then_inc(V_code, 1)
                    dve.wait_ge(V_code, q + 1)
                    for g in range(G):
                        v = dve.tensor_scalar(hot[:, bass.ds(q * G + g, 1), :], codes_f[:, 0:CODES],
                                              code[:, bass.ds(q * G + g, 1)], None, ALU.is_equal)
                    v.then_inc(D7, 1)
                if 3 in live:
                    q, b = i - 3, (k - 3) % 2
                    dve.wait_ge(P3, q + 1)
                    if not (first and q < 2):
                        dve.wait_ge(s_rec[b], (q - b) * 8)
                    for g in range(G):
                        v = dve.tensor_scalar(rec[:, b, g, 0:D], x1[:, b, g, :], mv1[:, b, g, 0:1], scale1[:, b, g:g + 1],
                                              ALU.subtract, ALU.mult)
                    v.then_inc(D6, 1)
                if 4 in live:
                    q, b = i - 4, k % 2
                    dve.wait_ge(M5, q + 1)
                    dve.tensor_tensor(hotR[:, :, :], bR[:, 0:G * CODES].rearrange("p (g c) -> p g c", g=G),
                                      hot[:, bass.ts(q, G), :], ALU.mult).then_inc(D8, 1)
                    dve.wait_ge(D8, q + 1)
                    dve.tensor_reduce(rank[:, bass.ts(q, G)], hotR[:, :, :], AX_X, ALU.add).then_inc(V_rank, 1)
                    dve.wait_ge(A6, q + 1)
                    dve.tensor_reduce(lsum[:, :], lexp[:, b, :, :], AX_X, ALU.add).then_inc(V_lsum, 1)
                    dve.wait_ge(V_lsum, q + 1)
                    dve.reciprocal(rec[:, b, :, 2 * D:2 * D + 1], lsum[:, :].unsqueeze(2)).then_inc(V_v1, 1)
                    dve.wait_ge(V_v1, q + 1)
                    dve.tensor_tensor(rec[:, b, :, 2 * D + 1:2 * D + 2], rec[:, b, :, 2 * D:2 * D + 1],
                                      lexp[:, b, :, 1:2], ALU.mult).then_inc(D9, 1)
            dve.wait_ge(s_w, 16 * SETUP_LOADS)
            dve.tensor_copy(part0[:, 0, :], bias_col[:, :]).then_inc(vs, 1)
            dve.wait_ge(vs, 1)
            dve.tensor_tensor(rest1[:, :], bias_col[:, :], part0[:, 0, :], ALU.subtract).then_inc(vs, 1)
            dve.wait_ge(vs, 2)
            dve.tensor_copy(part0[:, 1, :], rest1[:, :]).then_inc(vs, 1)
            dve.wait_ge(vs, 3)
            dve.tensor_tensor(rest2[:, :], rest1[:, :], part0[:, 1, :], ALU.subtract).then_inc(vs, 1)
            dve.wait_ge(vs, 4)
            dve.tensor_copy(part0[:, 2, :], rest2[:, :]).then_inc(V_part, 1)
            dve.wait_ge(s_c, 2)
            skewed(dve, NP, UNROLL, [0, 1, 2, 3, 4], body)

            dve.wait_ge(M6, NP)
            dve.wait_ge(s_c, 3)
            dve.wait_ge(V_rank, NP)
            dve.tensor_scalar(count_i[:, :], bR[:, 0:CODES], 127.0, None, ALU.add)
            dve.tensor_copy(rank_i[:, :], rank[:, :])
            dve.tensor_copy(token_f[:, :], token_i[:, :])
            dve.tensor_copy(part_f[:, :], part_i[:, :]).then_inc(vb, 1)
            dve.wait_ge(vb, 1)
            dve.tensor_scalar(tiles_i[:, :], count_i[:, :], 7, None, ALU.logical_shift_right)
            dve.tensor_scalar(rank_hi[:, :], rank_i[:, :], 7, None, ALU.logical_shift_right)
            dve.tensor_scalar(rank_lo[:, :], rank_i[:, :], 127, None, ALU.bitwise_and).then_inc(vb, 1)
            dve.wait_ge(vb, 2)
            dve.tensor_copy(tiles_f[:, :], tiles_i[:, :])
            dve.tensor_copy(place[:, :], rank_lo[:, :]).then_inc(vb, 1)
            dve.wait_ge(vb, 3)
            dve.tensor_tensor_scan(tile_end[:, :], ones_f[:, :], tiles_f[:, :], 0.0, ALU.mult, ALU.add).then_inc(vb, 1)
            dve.wait_ge(vb, 4)
            dve.tensor_tensor(start_h[:, :], tile_end[:, :], tiles_f[:, :], ALU.subtract)
            dve.tensor_scalar(ended[:, :], tile_end[:, :], part_f[:, 0:1], None, ALU.is_le).then_inc(vb, 1)
            dve.wait_ge(vb, 5)
            dve.tensor_reduce(tile_code[:, :], ended[:, :], AX_X, ALU.add).then_inc(vb, 1)
            dve.tensor_tensor(hot_start[:, :, :], hot[:, :, :],
                              start_h[:, :].unsqueeze(1).to_broadcast([128, 64, CODES]), ALU.mult).then_inc(vb, 1)
            dve.wait_ge(vb, 7)
            dve.tensor_scalar(tile_code[:, :], tile_code[:, :], float(CODES - 1), None, ALU.min).then_inc(B_col, 1)
            dve.tensor_reduce(start_of[:, :], hot_start[:, :, :], AX_X, ALU.add).then_inc(vb, 1)
            dve.wait_ge(vb, 8)
            dve.tensor_tensor(tile_of[:, :], start_of[:, :], rank_hi[:, :], ALU.add).then_inc(vb, 1)
            dve.wait_ge(vb, 9)

            def batch(i, k):
                free(dve, B_free, 1, i, 4)
                dve.tensor_scalar(is_place[:, k, :], codes_f[:, :], place[:, bass.ds(i, 1)], None, ALU.is_equal)
                dve.tensor_scalar(is_tile[:, k, :], codes_f[:, 0:TILES], tile_of[:, bass.ds(i, 1)],
                                  token_f[:, bass.ds(i, 1)], ALU.is_equal, ALU.mult).then_inc(B_place, 1)
            for i in range(4):
                batch(i, i)
            with dve.Fori(1, B // 4) as turn:
                for k in range(4):
                    batch(turn * 4 + k, k)

            dve.wait_ge(B_free, B)
            dve.tensor_scalar(empty[:, :], bO[:, 0:TILES], 0.5, SKIPPED, ALU.is_lt, ALU.mult)
            dve.tensor_scalar(gather_at[:, :], bO[:, 0:TILES], -1.0, 0.0, ALU.add, ALU.max)
            dve.tensor_copy(slots[:, :], bO[:, 0:TILES]).then_inc(vb, 1)
            dve.wait_ge(vb, 10)
            dve.scalar_tensor_tensor(scatter_at[:, :], slots[:, :], -1.0, empty[:, :], ALU.add, ALU.add).then_inc(B_idx, 1)
            dve.wait_ge(B_row, 1)
            dve.tensor_copy(tile_row[:, :], bP[0:1, 0:128]).then_inc(vb, 1)
            dve.wait_ge(vb, 11)
            dve.tensor_scalar(expert_row[:, 0, :], tile_row[:, :], 3, None, ALU.logical_shift_right)
            dve.tensor_scalar(expert_row[:, 1, :], tile_row[:, :], E - 1, None, ALU.bitwise_and).then_inc(B_rowdone, 1)

            def tile(i, k, live):
                if 4 in live:
                    t, r, b = i - 4, (k - 4) % TU, k % 2
                    dve.wait_ge(C4, t + 1)
                    free(dve, C5, 1, t, 2)
                    dve.scalar_tensor_tensor(boost[:, b, :], bP[:, 0:D], 0.5, tok[:, r, 0:D],
                                             ALU.mult, ALU.add).then_inc(C4b, 1)
                    dve.scalar_tensor_tensor(mixed[:, k % 4, :], bP[:, 0:D], tok[:, r, 2 * D:2 * D + 1], tok[:, r, 0:D],
                                             ALU.mult, ALU.add).then_inc(C4e, 1)
                if 3 in live:
                    t, b = i - 3, (k - 3) % 2
                    dve.wait_ge(C3, t + 1)
                    free(dve, C4, 1, t, 2)
                    dve.tensor_copy(hid1t[:, b].rearrange("p s t -> p (s t)"), bL[:, 0:H]).then_inc(C3e, 1)
                if 6 in live:
                    t, r, b = i - 6, (k - 6) % TU, k % 2
                    dve.wait_ge(C8, t + 1)
                    dve.scalar_tensor_tensor(z[:, b, :], bR[:, 0:D], tok[:, r, 2 * D + 1:2 * D + 2], mixed[:, (k - 6) % 4, :],
                                             ALU.mult, ALU.add).then_inc(C8e, 1)
                    dve.wait_ge(C8e, t + 1)
                    dve.bn_stats(statsz[:, :], z[:, b, :]).then_inc(V_zs, 1)
                    dve.wait_ge(V_zs, t + 1)
                    dve.nop(nofuse=True)
                    dve.bn_aggr(mvz[:, b, :], statsz[:, :]).then_inc(V_zm, 1)
                    dve.wait_ge(V_zm, t + 1)
                    dve.nop(nofuse=True)
                    dve.tensor_scalar(varz[:, b:b + 1], mvz[:, b, 1:2], EPS_LN, None, ALU.add).then_inc(C9, 1)
                if 5 in live:
                    t, b = i - 5, (k - 5) % 2
                    dve.wait_ge(C7, t + 1)
                    free(dve, C8, 1, t, 2)
                    dve.tensor_copy(hid2t[:, b].rearrange("p s t -> p (s t)"), bH[:, 0:H]).then_inc(C7e, 1)
                if 7 in live:
                    t, r, b, o = i - 7, (k - 7) % TU, (k - 7) % 2, (k - 7) % 4
                    free(dve, C11, 1, t, 1)
                    dve.scalar_tensor_tensor(y[:, :], z[:, b, :], mvz[:, b, 0:1], gamma_bc[:, :],
                                             ALU.subtract, ALU.mult).then_inc(V_y, 1)
                    dve.wait_ge(V_y, t + 1)
                    dve.wait_ge(C10, t + 1)
                    if not (isinstance(t, int) and t < 4):
                        dve.wait_ge(g_out[o], (t - o) * 4)
                    dve.scalar_tensor_tensor(row_out[:, o, :], y[:, :], scalez[:, b:b + 1], tok[:, r, D:2 * D],
                                             ALU.mult, ALU.add).then_inc(C11, 1)
            skewed(dve, TILES, TU, [3, 4, 5, 6, 7], tile)


_INS = ["x", "ctx_1024", "L0_xattn_q_w", "L0_xattn_k_w", "L0_xattn_norm_w", "L0_xattn_gate_w", "L0_xattn_gate_b",
        "L0_ffn_gate_W", "L0_ffn_gate_b", "L0_ffn_W1", "L0_ffn_b1", "L0_ffn_W2", "L0_ffn_b2", "L0_ffn_ln_gamma",
        "L0_ffn_ln_beta"]
_OUTS = [((B, S, D), "float32")]


def kernel(**inputs):
    import numpy as np
    import concourse.bacc as bacc
    from concourse.bass_utils import run_bass_kernel_spmd

    nc = bacc.Bacc("TRN2", target_bir_lowering=False, num_devices=1)
    arrays, args = {}, []
    for name in _INS:
        a = np.ascontiguousarray(inputs[name])
        arrays[f"in_{name}_dram"] = a
        args.append(nc.dram_tensor(f"in_{name}_dram", a.shape, mybir.dt.from_np(a.dtype), kind="ExternalInput").ap())
    for n, (shape, dtype) in enumerate(_OUTS):
        args.append(nc.dram_tensor(f"out_{n}_dram", shape, mybir.dt.from_np(np.dtype(dtype)), kind="ExternalOutput").ap())
    program(nc, *args)
    r = run_bass_kernel_spmd(nc, [arrays], core_ids=[0])
    return r.results[0]["out_0_dram"]
```

```python
from contextlib import ExitStack

import concourse.bass as bass
from concourse import mybir

F32 = mybir.dt.float32
BF16 = mybir.dt.bfloat16
U32 = mybir.dt.uint32
I32 = mybir.dt.int32
ALU = mybir.AluOpType
ACT = mybir.ActivationFunctionType
AX_X = mybir.AxisListType.X

B, S, D = 64, 128, 128
SC = 77
E, H = 8, 256
HH = H // 128
G = 2
NP = B // G
CODES = E * E
TILES = 120
T = S + SC
REC = 2 * D + 2
EPS_LN, EPS_RMS = 1e-5, 1e-6
NEG = -1.0e30
UNROLL = 4
TG = 2
UNITS = TILES // TG
RING = 8
ROWS = 4
SKIPPED = 1.0e6
WE = H + HH * D


def skewed(engine, count, unroll, lags, body):
    last = max(lags)
    first = -(-last // unroll) * unroll
    for i in range(first):
        body(i, i % unroll, [l for l in lags if i >= l])
    end = first + (count - first) // unroll * unroll
    with engine.Fori(first // unroll, end // unroll) as turn:
        for k in range(unroll):
            body(turn * unroll + k, k, lags)
    for i in range(end, count + last):
        body(i, i % unroll, [l for l in lags if 0 <= i - l < count])


def free(engine, semaphore, per, unit, depth):
    if isinstance(unit, int) and unit < depth:
        return
    engine.wait_ge(semaphore, (unit - (depth - 1)) * per)


def program(nc, x, ctx, q_w, k_w, norm_w, gate_w, gate_b, router_w, router_b, W1, b1, W2, b2,
            gamma, beta, out):
    stack = ExitStack()
    with stack:
        def sb(name, shape, dt=F32):
            return stack.enter_context(nc.sbuf_tensor(name, shape, dt))

        def sem(name):
            return stack.enter_context(nc.semaphore(name))

        out_rows = out.rearrange("b s d -> (b s) d")
        records = nc.dram_tensor("records", [B * S, REC], F32).ap()

        ident = sb("ident", [128, 128])
        ident_h = sb("ident_h", [128, 128], BF16)
        mask_h = sb("mask_h", [128, 128], BF16)
        before_h = sb("before_h", [128, 128], BF16)
        rest_h = sb("rest_h", [128, 128], BF16)
        ones_h = sb("ones_h", [128, 128], BF16)
        zeros_h = sb("zeros_h", [128, 128], BF16)
        codes_i = sb("codes_i", [128, 128], I32)
        codes_f = sb("codes_f", [128, 128])
        minus_half = sb("minus_half", [128, 2 * G])
        qw = sb("qw", [128, D])
        kw = sb("kw", [128, D])
        gw = sb("gw", [128, D])
        score_m = sb("score_m", [128, D])
        gwT = sb("gwT", [128, D])
        w_bc = sb("w_bc", [128, G, D])
        beta_bc = sb("beta_bc", [128, G, D])
        gamma_bc = sb("gamma_bc", [128, D])
        rw = sb("rw", [128, E])
        rb_bc = sb("rb_bc", [128, G, E])
        We = sb("We", [128, E, WE])
        x_in = sb("x_in", [128, 4, G, D])
        c_in = sb("c_in", [SC, 4, G, D])
        stats = sb("stats", [128, G, 6])
        mv = sb("mv", [128, 2, G, 2])
        var_ab = sb("var_ab", [128, 2, 2, G])
        scale = sb("scale", [128, 2, 3, G])
        shift = sb("shift", [128, 2, 3, G])
        normed = sb("normed", [128, 2, G, D])
        h0_half = sb("h0_half", [128, 4, G, D])
        vw = sb("vw", [128, 4, G, D])
        xh = sb("xh", [128, 4, G, D])
        tT = sb("tT", [128, 2, 2, G, D])
        cA = sb("cA", [128, 2, G * SC + G * S])
        tanh_z = sb("tanh_z", [128, 4, G, D])
        negmax = sb("negmax", [128, 2, G])
        prob = sb("prob", [128, 2, G, T])
        denom = sb("denom", [128, 2, G])
        rden = sb("rden", [128, G])
        pTs = sb("pTs", [128, 2, G, S])
        pTc = sb("pTc", [SC, 2, G, S])
        diff = sb("diff", [128, G, D])
        gated = sb("gated", [128, 2, G, D])
        x1 = sb("x1", [128, 2, G, D])
        stats1 = sb("stats1", [128, G, 6])
        mv1 = sb("mv1", [128, 2, G, 2])
        var1 = sb("var1", [128, 2, G])
        scale1 = sb("scale1", [128, 2, G])
        shift1 = sb("shift1", [128, 2, G])
        rec = sb("rec", [128, 4, G, REC])
        h1T = sb("h1T", [128, 2, G, S])
        lg = sb("lg", [128, G, E])
        top = sb("top", [128, G, E])
        topi = sb("topi", [128, G, E], U32)
        ldiff = sb("ldiff", [128, 2, G, E])
        lexp = sb("lexp", [128, 2, G, E])
        lsum = sb("lsum", [128, G])
        code = sb("code", [128, 64])
        hot = sb("hot", [128, 64, CODES], BF16)
        hotR = sb("hotR", [128, G, CODES])
        rank = sb("rank", [128, 64])

        bias_col = sb("bias_col", [128, 25])
        part0 = sb("part0", [128, 3, 25], BF16)
        rest1 = sb("rest1", [128, 25])
        rest2 = sb("rest2", [128, 25])
        b1s = sb("b1s", [3, E, H], BF16)
        b2s = sb("b2s", [3, E, D], BF16)
        gbs = sb("gbs", [3, D], BF16)
        count_i = sb("count_i", [128, CODES], I32)
        tiles_i = sb("tiles_i", [128, CODES], I32)
        tiles_f = sb("tiles_f", [128, CODES])
        tile_end = sb("tile_end", [128, CODES])
        ones_f = sb("ones_f", [128, CODES])
        start_h = sb("start_h", [128, CODES], BF16)
        hot_start = sb("hot_start", [128, 64, CODES], BF16)
        start_of = sb("start_of", [128, 64])
        rank_i = sb("rank_i", [128, 64], I32)
        rank_hi = sb("rank_hi", [128, 64], I32)
        rank_lo = sb("rank_lo", [128, 64], I32)
        tile_of = sb("tile_of", [128, 64])
        place = sb("place", [128, 64])
        token_i = sb("token_i", [128, 64], I32)
        token_f = sb("token_f", [128, 64])
        part_i = sb("part_i", [128, 1], I32)
        part_f = sb("part_f", [128, 1])
        is_place = sb("is_place", [128, 4, 128])
        is_tile = sb("is_tile", [128, 4, TILES])
        ended = sb("ended", [128, CODES])
        tile_code = sb("tile_code", [128, 1])
        tile_row = sb("tile_row", [1, 128], I32)
        plan = sb("plan", [1, UNITS + 8, 4, TG], I32)
        slots = sb("slots", [128, TILES])
        empty = sb("empty", [128, TILES])
        gather_at = sb("gather_at", [128, TILES], U32)
        scatter_at = sb("scatter_at", [128, TILES], U32)
        gather_now = sb("gather_now", [128, RING * TG], U32)
        scatter_now = sb("scatter_now", [128, RING * TG], U32)
        tok = sb("tok", [128, RING, TG, REC])
        w_up1 = sb("w_up1", [128, 2, TG, H])
        w_up2 = sb("w_up2", [128, 2, TG, H])
        h1t = sb("h1t", [128, 2, TG, 128])
        hid1 = sb("hid1", [128, 2, TG, HH, 128])
        boost = sb("boost", [128, 2, TG, D])
        mixed = sb("mixed", [128, 2, TG, D])
        boostt = sb("boostt", [128, 2, TG, 128])
        hid2 = sb("hid2", [128, 2, TG, HH, 128])
        z = sb("z", [128, 2, TG, D])
        statsz = sb("statsz", [128, 2, TG, 6])
        mvz = sb("mvz", [128, 2, TG, 2])
        varz = sb("varz", [128, 2, TG])
        scalez = sb("scalez", [128, 2, TG])
        y = sb("y", [128, TG, D])
        row_out = sb("row_out", [128, ROWS, TG, D])

        def bank(name):
            return stack.enter_context(nc.psum_tensor(name, [128, 512], F32))

        bT, bC, bL, bP, bZ, bO, bH, bR = [bank(f"bank{n}") for n in range(8)]

        s_w, s_bias, s_norm_w, s_qkg = sem("weights_in"), sem("biases_in"), sem("norm_weight_in"), sem("qkg_in")
        lg_ready, weight1_ready = sem("lg_ready"), sem("weight1_ready")
        s_we = sem("experts_in")
        s_c = sem("constants")
        s_setup_pe = sem("setup_pe")
        s_setup_act = sem("setup_act")
        x_ready = [sem(f"x_ready{k}") for k in range(4)]
        stored = [sem(f"record_stored{k}") for k in range(4)]
        stats_ready, mv_ready, var_ready = sem("stats_ready"), sem("mv_ready"), sem("var_ready")
        scales_ready, shift_ready, coefficients_ready = sem("scales_ready"), sem("shift_ready"), sem("coefficients_ready")
        tokens_normed, vw_ready, tokens_transposed = sem("tokens_normed"), sem("vw_ready"), sem("tokens_transposed")
        tT_ready, scoremix_done, gate_done = sem("tT_ready"), sem("scoremix_done"), sem("gate_done")
        cA_ready, tanh_ready, scores_done = sem("cA_ready"), sem("tanh_ready"), sem("scores_done")
        max_ready, prob_ready, prob_transposed = sem("max_ready"), sem("prob_ready"), sem("prob_transposed")
        pT_ready, attended, rden_ready = sem("pT_ready"), sem("attended"), sem("rden_ready")
        diff_ready, gated_ready, x1_ready = sem("diff_ready"), sem("gated_ready"), sem("x1_ready")
        stats1_ready, mv1_ready, var1_ready = sem("stats1_ready"), sem("mv1_ready"), sem("var1_ready")
        scale1_ready, shift1_ready, h1_ready = sem("scale1_ready"), sem("shift1_ready"), sem("h1_ready")
        x1b_ready, h1_transposed, h1T_ready = sem("x1b_ready"), sem("h1_transposed"), sem("h1T_ready")
        router_done, top_ready, topi_ready = sem("router_done"), sem("top_ready"), sem("topi_ready")
        ldiff_ready, lexp_ready, code_ready = sem("ldiff_ready"), sem("lexp_ready"), sem("code_ready")
        hot_ready, rank_done, hotR_ready = sem("hot_ready"), sem("rank_done"), sem("hotR_ready")
        rank_ready, rank_base_done, lsum_ready = sem("rank_ready"), sem("rank_base_done"), sem("lsum_ready")
        weights_ready = sem("weights_ready")
        V_part = sem("v_part")
        vs = sem("v_setup")
        s_bout, s_bin = sem("bias_parts_out"), sem("bias_parts_in")
        vb = sem("v_sorting")
        B_place, B_free, B_done = sem("place_ready"), sem("place_used"), sem("slots_done")
        B_col, B_row, B_rowdone = sem("tile_code_ready"), sem("tile_row_done"), sem("expert_row_ready")
        B_idx = sem("indices_ready")
        gather_cols, scatter_cols = sem("gather_columns_ready"), sem("scatter_columns_ready")
        gathered = [sem(f"gathered{n}") for n in range(RING * TG)]
        scattered = [sem(f"scattered{n}") for n in range(ROWS * TG)]
        records_transposed, recordsT_ready = sem("records_transposed"), sem("recordsT_ready")
        up1_done, hid1_ready = sem("up1_done"), sem("hid1_ready")
        out1_done, boost_ready = sem("out1_done"), sem("boost_ready")
        boostT_done, boostT_ready = sem("boost_transposed"), sem("boostt_ready")
        up2_done, hid2_ready = sem("up2_done"), sem("hid2_ready")
        out2_done, z_ready, zstats_ready, zmv_ready, varz_ready = (sem("out2_done"), sem("z_ready"), sem("zstats_ready"),
                                                                   sem("zmv_ready"), sem("varz_ready"))
        scalez_ready, y_ready, rows_ready = sem("scalez_ready"), sem("y_ready"), sem("rows_ready")

        block = stack.enter_context(nc.Block())

        x_v = x.rearrange("(n g) s d -> n s g d", g=G)
        c_v = ctx.rearrange("(n g) s d -> n s g d", g=G)
        rec_v = records.rearrange("(n g s) r -> n s g r", g=G, s=S)
        SETUP_LOADS = 2 * G + 2
        parts = nc.dram_tensor("bias_parts", [3, 128 * 25], BF16).ap()
        BIAS = ((0, E * H // 128), (E * H // 128, E * D // 128), (24, 1))

        @block.sync
        def _(sp):
            def load(i, k):
                if not (isinstance(i, int) and i < 4):
                    sp.wait_ge(tokens_normed, i - 3)
                    sp.wait_ge(attended, i - 3)
                sp.dma_start(x_in[:, k, :, :], x_v[i]).then_inc(x_ready[k], 16)
                sp.dma_start(c_in[:, k, :, :], c_v[i]).then_inc(x_ready[k], 16)

            load(0, 0)
            for (at, n), src in zip(BIAS, (b1.rearrange("e (a f) -> (e a) f", f=16), b2.rearrange("e (a f) -> (e a) f", f=8),
                                          gate_b.rearrange("(p a) -> p a", a=1))):
                sp.dma_start(bias_col[:, at:at + n], src).then_inc(s_bias, 16)
            row = lambda v: v.rearrange("(a n) -> a n", a=1).to_broadcast([128, v.shape[0]])
            for g in range(G):
                sp.dma_start(w_bc[:, g, :], row(norm_w)).then_inc(s_norm_w, 16)
            load(1, 1)
            for g in range(G):
                sp.dma_start(rb_bc[:, g, :], row(router_b)).then_inc(s_w, 16)
                sp.dma_start(beta_bc[:, g, :], row(beta)).then_inc(s_w, 16)
            sp.dma_start(rw[:, :], router_w).then_inc(s_w, 16)
            sp.dma_start(gamma_bc[:, :], row(gamma)).then_inc(s_w, 16)
            sp.wait_ge(V_part, 1)
            for at, n in BIAS[::-1]:
                sp.dma_start(parts[:, 128 * at:128 * (at + n)].rearrange("t (p f) -> p t f", f=n),
                             part0[:, :, at:at + n], allow_slow_non_contiguous=n == 1).then_inc(s_bout, 16)
            sp.wait_ge(s_bout, 48)
            for (at, n), dst in zip(BIAS, (b1s[:, :, :].rearrange("t e h -> t (e h)"),
                                           b2s[:, :, :].rearrange("t e d -> t (e d)"), gbs[:, :])):
                sp.dma_start(dst, parts[:, 128 * at:128 * (at + n)]).then_inc(s_bin, 16)

            def body(i, k, live):
                if 0 in live and not (isinstance(i, int) and i < 2):
                    load(i, k)
                if isinstance(i, int) and i == 4:
                    for e in range(E):
                        sp.dma_start(We[:, e, 0:H], W1[e]).then_inc(s_we, 16)
                        sp.dma_start(We[:, e, H:WE].rearrange("p (s d) -> p s d", s=HH),
                                     W2[e].rearrange("(s p) d -> p s d", p=128)).then_inc(s_we, 16)
                if 7 in live:
                    q, r = i - 7, (k - 7) % 4
                    sp.wait_ge(h1_ready, q + 1)
                    sp.wait_ge(x1b_ready, q + 1)
                    sp.wait_ge(weights_ready, q + 1)
                    sp.dma_start(rec_v[q], rec[:, r, :, :]).then_inc(stored[r], 16)
            skewed(sp, NP, UNROLL, [0, 7], body)
            for r in range(4):
                sp.wait_ge(stored[r], 16 * (NP // 4))

        @block.gpsimd
        def _(pool):
            pool.memset(ident[:, :], 0.0)
            pool.memset(ident_h[:, :], 0.0)
            pool.memset(mask_h[:, :], 0.0)
            pool.memset(before_h[:, :], 0.0)
            pool.memset(rest_h[:, :], 0.0)
            pool.memset(ones_h[:, :], 1.0)
            pool.memset(zeros_h[:, :], 0.0)
            pool.memset(minus_half[:, :], -0.5)
            pool.iota(codes_i[:, :], [[1, 128]], base=0, channel_multiplier=0).then_inc(s_c, 1)
            pool.wait_ge(s_c, 1)
            for m in (ident, ident_h):
                pool.affine_select(out=m[:, :], in_=m[:, :], compare_op=ALU.not_equal, fill=1.0, base=0,
                                   pattern=[[-1, 128]], channel_multiplier=1)
            pool.affine_select(out=mask_h[:, :], in_=mask_h[:, :], compare_op=ALU.is_ge, fill=NEG, base=0,
                               pattern=[[-1, 128]], channel_multiplier=1)
            pool.affine_select(out=before_h[:, :], in_=before_h[:, :], compare_op=ALU.is_ge, fill=1.0, base=0,
                               pattern=[[-1, 128]], channel_multiplier=1)
            pool.affine_select(out=rest_h[:, :], in_=rest_h[:, :], compare_op=ALU.is_gt, fill=1.0, base=0,
                               pattern=[[1, 128]], channel_multiplier=-1)
            pool.tensor_copy(codes_f[:, :], codes_i[:, :]).then_inc(s_c, 1)
            pool.iota(token_i[:, :], [[S, B]], base=1, channel_multiplier=1)
            pool.iota(part_i[:, :], [[0, 1]], base=0, channel_multiplier=1)
            pool.memset(plan[:, :, :, :], 0)
            pool.memset(ones_f[:, :], 1.0).then_inc(s_c, 1)

            def body(i, k, live):
                if 1 in live:
                    q, r, b = i - 1, (k - 1) % 4, (k - 1) % 2
                    if isinstance(q, int) and q == 0:
                        pool.wait_ge(s_norm_w, 16 * G)
                    pool.wait_ge(tokens_normed, q + 1)
                    pool.tensor_tensor(vw[:, r, :, :], normed[:, b, :, :], w_bc[:, :, :], ALU.mult).then_inc(vw_ready, 1)
                if 0 in live:
                    q, b = i, k % 2
                    pool.wait_ge(var_ready, q + 1)
                    pool.tensor_tensor(scale[:, b, 0:2, :].rearrange("p a g -> p (a g)"),
                                       var_ab[:, b].rearrange("p a g -> p (a g)"),
                                       minus_half[:, :], ALU.pow).then_inc(scales_ready, 1)
                if 3 in live:
                    q, r, b = i - 3, (k - 3) % 4, (k - 3) % 2
                    pool.wait_ge(gated_ready, q + 1)
                    pool.tensor_tensor(x1[:, b, :, :], gated[:, b, :, :], xh[:, r, :, :], ALU.add).then_inc(x1_ready, 1)
                    if isinstance(q, int) and q == 0:
                        pool.wait_ge(s_w, 16 * SETUP_LOADS)
                    pool.wait_ge(x1_ready, q + 1)
                    if not (isinstance(q, int) and q < 4):
                        pool.wait_ge(stored[r], (q - r) * 4)
                    pool.tensor_tensor(rec[:, r, :, D:2 * D], x1[:, b, :, :], beta_bc[:, :, :], ALU.add).then_inc(x1b_ready, 1)
                    pool.wait_ge(var1_ready, q + 1)
                    pool.tensor_tensor(scale1[:, b, :], var1[:, b, :], minus_half[:, 0:G], ALU.pow).then_inc(scale1_ready, 1)
            skewed(pool, NP, UNROLL, [0, 1, 3], body)

            pool.wait_ge(B_idx, 1)
            for r in range(4):
                pool.wait_ge(stored[r], 16 * (NP // 4))

            def unit(i, k, live):
                if 6 in live:
                    u, b = i - 6, k % 2
                    pool.wait_ge(varz_ready, u + 1)
                    pool.tensor_tensor(scalez[:, b, :], varz[:, b, :], minus_half[:, 0:TG], ALU.pow).then_inc(scalez_ready, 1)
                if 7 in live:
                    u, b = i - 7, (k - 7) % ROWS
                    pool.wait_ge(rows_ready, u + 1)
                    pool.nop(nofuse=True)
                    for g in range(TG):
                        n = (k - 7) % RING * TG + g
                        pool.indirect_dma_start(out_rows, bass.IndirectOffsetOnAxis(ap=scatter_now[:, n:n + 1], axis=0),
                                                row_out[:, b, g, :], None, bounds_check=B * S - 1, oob_is_err=False
                                                ).then_inc(scattered[b * TG + g], 16)
                if 1 in live:
                    u, r = i - 1, (k - 1) % RING
                    pool.wait_ge(gather_cols, u + 1)
                    free(pool, rows_ready, 1, u, RING)
                    pool.nop(nofuse=True)
                    for g in range(TG):
                        n = r * TG + g
                        pool.indirect_dma_start(tok[:, r, g, :], None, records,
                                                bass.IndirectOffsetOnAxis(ap=gather_now[:, n:n + 1], axis=0)
                                                ).then_inc(gathered[n], 16)
            skewed(pool, UNITS, RING, [1, 6, 7], unit)
            for n in range(ROWS * TG):
                pool.wait_ge(scattered[n], 16 * (UNITS // ROWS))

        @block.tensor
        def _(pe):
            pe.wait_ge(s_c, 2)
            pe.matmul(bR[:, 0:G * CODES], ones_h[:, :], zeros_h[:, :], start=True, stop=False, skip_group_check=True)
            pe.wait_ge(s_qkg, 48)
            pe.matmul(bL[:, 0:128], qw[:, :], kw[:, :], start=True, stop=True)
            pe.transpose(bL[:, 128:256], gw[:, :], ident[:, :]).then_inc(s_setup_pe, 1)

            def body(i, k, live):
                first = isinstance(i, int)
                if 1 in live:
                    q, r = i - 1, (k - 1) % 4
                    pe.wait_ge(x_ready[r], (q - r) * 8 + 32)
                    for g in range(G):
                        pe.transpose(bC[:, g * SC:(g + 1) * SC], c_in[:, r, g, :], ident[0:SC, 0:SC])
                    pe.wait_ge(tokens_normed, q + 1)
                    for g in range(G):
                        pe.transpose(bT[:, (G + g) * S:(G + g + 1) * S], h0_half[:, r, g, :], ident[:, :])
                    pe.wait_ge(vw_ready, q + 1)
                    for g in range(G):
                        mm = pe.transpose(bT[:, g * S:(g + 1) * S], vw[:, r, g, :], ident[:, :])
                    mm.then_inc(tokens_transposed, 1)
                if 4 in live:
                    q, r = i - 4, k % 4
                    pe.wait_ge(h1_ready, q + 1)
                    for g in range(G):
                        mm = pe.transpose(bH[:, g * S:(g + 1) * S], rec[:, r, g, 0:D], ident[:, :])
                    mm.then_inc(h1_transposed, 1)
                if 1 in live:
                    q, b = i - 1, (k - 1) % 2
                    if first and q == 0:
                        pe.wait_ge(s_setup_act, 1)
                    pe.wait_ge(tT_ready, q + 1)
                    pe.matmul(bC[:, G * SC:G * SC + G * S], score_m[:, :],
                              tT[:, b, 0, :, :].rearrange("p g s -> p (g s)"), start=True, stop=True).then_inc(scoremix_done, 1)
                    if first and q == 0:
                        pe.wait_ge(s_bin, 48)
                    for g in range(G):
                        pe.matmul(bZ[:, g * D:(g + 1) * D], tT[:, b, 1, g, :], gwT[:, :], start=True, stop=False)
                        mm = pe.matmul(bZ[:, g * D:(g + 1) * D], ones_h[0:3, :], gbs[:, :], start=False, stop=True)
                    mm.then_inc(gate_done, 1)
                if 2 in live:
                    q, b = i - 2, k % 2
                    pe.wait_ge(prob_ready, q + 1)
                    for g in range(G):
                        pe.transpose(bP[:, g * S:(g + 1) * S], prob[:, b, g, 0:S], ident[:, :])
                        mm = pe.transpose(bP[0:SC, (G + g) * S:(G + g + 1) * S], prob[:, b, g, S:T], ident[:, :])
                    mm.then_inc(prob_transposed, 1)
                if 1 in live:
                    q, b = i - 1, (k - 1) % 2
                    pe.wait_ge(cA_ready, q + 1)
                    for g in range(G):
                        A = cA[:, b, G * SC + g * S:G * SC + (g + 1) * S]
                        o = g * 256
                        pe.matmul(bL[:, o:o + S], A, tT[:, b, 0, g, :], start=True, stop=False)
                        pe.matmul(bL[:, o:o + S], ident_h[:, :], mask_h[:, :], start=False, stop=True)
                        mm = pe.matmul(bL[:, o + S:o + T], A, cA[:, b, g * SC:(g + 1) * SC], start=True, stop=True)
                    mm.then_inc(scores_done, 1)
                if 2 in live:
                    q, r, b = i - 2, (k - 2) % 4, k % 2
                    free(pe, diff_ready, 1, q, 1)
                    pe.wait_ge(pT_ready, q + 1)
                    for g in range(G):
                        pe.matmul(bO[:, g * D:(g + 1) * D], pTs[:, b, g, :], vw[:, r, g, :], start=True, stop=False)
                        mm = pe.matmul(bO[:, g * D:(g + 1) * D], pTc[:, b, g, :], c_in[:, r, g, :], start=False, stop=True)
                    mm.then_inc(attended, 1)
                if 6 in live:
                    q = i - 6
                    pe.wait_ge(hotR_ready, q + 1)
                    pair_hot = hot[:, bass.ts(q, G), :].rearrange("p g c -> p (g c)")
                    pe.matmul(bR[:, 0:G * CODES], rest_h[:, :], pair_hot, start=False, stop=False,
                              skip_group_check=True)
                    pe.matmul(bR[:, 0:CODES], ones_h[:, :], pair_hot[:, CODES:2 * CODES], start=False, stop=False,
                              skip_group_check=True).then_inc(rank_base_done, 1)
                if 5 in live:
                    q = i - 5
                    pe.wait_ge(hot_ready, q + 1)
                    pair_hot = hot[:, bass.ts(q, G), :].rearrange("p g c -> p (g c)")
                    pe.matmul(bR[:, 0:G * CODES], before_h[:, :], pair_hot, start=False,
                              stop=False, skip_group_check=True)
                    pe.matmul(bR[:, CODES:2 * CODES], ones_h[:, :], pair_hot[:, 0:CODES], start=False, stop=False,
                              skip_group_check=True).then_inc(rank_done, 1)
                if 4 in live:
                    q, b = i - 4, k % 2
                    pe.wait_ge(h1T_ready, q + 1)
                    for g in range(G):
                        mm = pe.matmul(bO[:, G * D + g * E:G * D + (g + 1) * E], h1T[:, b, g, :], rw[:, :],
                                       start=True, stop=True)
                    mm.then_inc(router_done, 1)
            skewed(pe, NP, UNROLL, [1, 2, 4, 5, 6], body)

            pe.wait_ge(diff_ready, NP)

            def batch(i, k, live):
                pe.wait_ge(B_place, i + 1)
                pe.matmul(bO[:, 0:TILES], is_place[:, k, :], is_tile[:, k, :],
                          start=isinstance(i, int) and i == 0, stop=isinstance(i, int) and i == B - 1,
                          skip_group_check=True).then_inc(B_free, 1)
            for i in range(4):
                batch(i, i, None)
            with pe.Fori(1, B // 4 - 1) as turn:
                for k in range(4):
                    batch(turn * 4 + k, k, None)
            for i in range(B - 4, B):
                batch(i, i % 4, None)
            pe.wait_ge(B_col, 1)
            pe.matmul(bP[0:1, 0:128], tile_code[:, :], ident[:, :], start=True, stop=True).then_inc(B_row, 1)

            pe.wait_ge(s_we, 16 * 2 * E)
            pe.wait_ge(B_rowdone, 1)

            registers = [pe.alloc_register(f"pe_expert{n}") for n in range(4 * TG)]

            def up(dst, w, xt, e):
                for s in range(HH):
                    pe.matmul(dst[:, s * 128:(s + 1) * 128], w[:, s * 128:(s + 1) * 128], xt, start=True, stop=False)
                    mm = pe.matmul(dst[:, s * 128:(s + 1) * 128], b1s[:, bass.ds(e, 1), s * 128:(s + 1) * 128],
                                   ones_h[0:3, :], start=False, stop=True)
                return mm

            def down(dst, hT, e):
                for s in range(HH):
                    pe.matmul(dst, hT[:, s, :], We[:, bass.ds(e, 1), H + s * D:H + (s + 1) * D], start=s == 0, stop=False)
                return pe.matmul(dst, ones_h[0:3, :], b2s[:, bass.ds(e, 1), :], start=False, stop=True)

            def unit(i, k, live):
                pe.load(registers, plan[0:1, bass.ds(i, 1), :, :].rearrange("p u n g -> p (u n g)"))
                e = [pe.snap(r, min_val=0, max_val=E - 1) for r in registers]
                if 3 in live:
                    u, r = i - 3, (k - 3) % RING
                    for g in range(TG):
                        pe.wait_ge(gathered[r * TG + g], (u - r) * (16 // RING) + 16)
                        mm = pe.transpose(bT[:, g * 128:(g + 1) * 128], tok[:, r, g, 0:D], ident[:, :])
                    mm.then_inc(records_transposed, 1)
                if 4 in live:
                    u, b = i - 4, (k - 4) % 2
                    pe.wait_ge(hid1_ready, u + 1)
                    for g in range(TG):
                        mm = down(bP[:, g * D:(g + 1) * D], hid1[:, b, g], e[2 * TG + g])
                    mm.then_inc(out1_done, 1)
                if 3 in live:
                    u, b = i - 3, (k - 3) % 2
                    pe.wait_ge(recordsT_ready, u + 1)
                    for g in range(TG):
                        mm = up(bC[:, g * H:(g + 1) * H], w_up1[:, b, g, :], h1t[:, b, g, :], e[g])
                    mm.then_inc(up1_done, 1)
                if 5 in live:
                    u, b2 = i - 5, (k - 5) % 2
                    pe.wait_ge(hid2_ready, u + 1)
                    free(pe, z_ready, TG, u, 1)
                    down(bR[:, 0:D], hid2[:, b2, 0], e[3 * TG])
                if 4 in live:
                    u, b = i - 4, (k - 4) % 2
                    pe.wait_ge(boost_ready, u + 1)
                    for g in range(TG):
                        mm = pe.transpose(bZ[:, g * 128:(g + 1) * 128], boost[:, b, g, :], ident[:, :])
                    mm.then_inc(boostT_done, 1)
                if 5 in live:
                    down(bR[:, D:2 * D], hid2[:, b2, 1], e[3 * TG + 1]).then_inc(out2_done, 1)
                if 4 in live:
                    u, b = i - 4, (k - 4) % 2
                    pe.wait_ge(boostT_ready, u + 1)
                    for g in range(TG):
                        mm = up(bO[:, g * H:(g + 1) * H], w_up2[:, b, g, :], boostt[:, b, g, :], e[TG + g])
                    mm.then_inc(up2_done, 1)
            skewed(pe, UNITS, RING, [3, 4, 5], unit)

        @block.scalar
        def _(act):
            for dst, src in ((qw, q_w), (kw, k_w), (gw, gate_w)):
                act.dma_start(dst[:, :], src).then_inc(s_qkg, 16)

            def body(i, k, live):
                if isinstance(i, int) and i == 1:
                    act.wait_ge(s_setup_pe, 1)
                    act.activation(score_m[:, :], bL[:, 0:128], ACT.Copy, scale=D ** -0.5)
                    act.activation(gwT[:, :], bL[:, 128:256], ACT.Copy).then_inc(s_setup_act, 1)
                if 4 in live:
                    q, r, b = i - 4, k % 4, k % 2
                    act.wait_ge(shift1_ready, q + 1)
                    for g in range(G):
                        a = act.activation(rec[:, r, g, 0:D], x1[:, b, g, :], ACT.Identity,
                                           bias=shift1[:, b, g:g + 1], scale=scale1[:, b, g:g + 1])
                    a.then_inc(h1_ready, 1)
                if 1 in live:
                    q, b = i - 1, (k - 1) % 2
                    act.wait_ge(tokens_transposed, q + 1)
                    act.activation(tT[:, b].rearrange("p a g s -> p (a g s)"), bT[:, :], ACT.Copy).then_inc(tT_ready, 1)
                if 2 in live:
                    q, b = i - 2, k % 2
                    act.wait_ge(max_ready, q + 1)
                    for g in range(G):
                        a = act.activation(prob[:, b, g, :], bL[:, g * 256:g * 256 + T], ACT.Exp,
                                           bias=negmax[:, b, g:g + 1], accum_out=denom[:, b, g:g + 1])
                    a.then_inc(prob_ready, 1)
                if 1 in live:
                    q, b = i - 1, (k - 1) % 2
                    act.wait_ge(scoremix_done, q + 1)
                    act.activation(cA[:, b, :], bC[:, 0:G * SC + G * S], ACT.Copy).then_inc(cA_ready, 1)
                if 2 in live:
                    q, b = i - 2, k % 2
                    act.wait_ge(prob_transposed, q + 1)
                    act.activation(pTs[:, b].rearrange("p g s -> p (g s)"), bP[:, 0:G * S], ACT.Copy, scale=0.5)
                    act.activation(pTc[:, b].rearrange("p g s -> p (g s)"), bP[0:SC, G * S:2 * G * S],
                                   ACT.Copy, scale=0.5).then_inc(pT_ready, 1)
                if 4 in live:
                    q, b = i - 4, k % 2
                    act.wait_ge(h1_transposed, q + 1)
                    act.activation(h1T[:, b].rearrange("p g s -> p (g s)"), bH[:, 0:G * S], ACT.Copy).then_inc(h1T_ready, 1)
                if 1 in live:
                    q, r = i - 1, (k - 1) % 4
                    act.wait_ge(gate_done, q + 1)
                    act.activation(tanh_z[:, r].rearrange("p g d -> p (g d)"), bZ[:, 0:G * D], ACT.Tanh).then_inc(tanh_ready, 1)
                if 5 in live:
                    q, b = i - 5, (k - 5) % 2
                    act.wait_ge(ldiff_ready, q + 1)
                    act.activation(lexp[:, b].rearrange("p g e -> p (g e)"), ldiff[:, b].rearrange("p g e -> p (g e)"),
                                   ACT.Exp).then_inc(lexp_ready, 1)
                if 0 in live:
                    q, r, b = i, k, k % 2
                    act.wait_ge(coefficients_ready, q + 1)
                    for g in range(G):
                        for n, dst in enumerate((normed[:, b, g, :], h0_half[:, r, g, :], xh[:, r, g, :])):
                            a = act.activation(dst, x_in[:, r, g, :], ACT.Identity,
                                               bias=shift[:, b, n, g:g + 1], scale=scale[:, b, n, g:g + 1])
                    a.then_inc(tokens_normed, 1)
            skewed(act, NP, UNROLL, [0, 1, 2, 4, 5], body)

            act.wait_ge(s_we, 16 * 2 * E)
            act.wait_ge(B_rowdone, 1)

            registers = [act.alloc_register(f"act_expert{n}") for n in range(2 * TG)]

            def weights(dst, e):
                return act.activation(dst, We[:, bass.ds(e, 1), 0:H], ACT.Copy)

            def unit(i, k, live):
                act.load(registers, plan[0:1, bass.ds(i + 1, 1), 0:2, :].rearrange("p u n g -> p (u n g)"))
                e = [act.snap(r, min_val=0, max_val=E - 1) for r in registers]
                if 3 in live:
                    u, b = i - 3, (k - 3) % 2
                    act.wait_ge(records_transposed, u + 1)
                    act.activation(h1t[:, b].rearrange("p g t -> p (g t)"), bT[:, 0:TG * 128], ACT.Copy).then_inc(recordsT_ready, 1)
                if 2 in live:
                    b = k % 2
                    for g in range(TG):
                        weights(w_up1[:, b, g, :], e[g])
                if 3 in live:
                    u, b = i - 3, (k - 3) % 2
                    act.wait_ge(up1_done, u + 1)
                    act.activation(hid1[:, b].rearrange("p g s t -> p (g s t)"), bC[:, :], ACT.Relu).then_inc(hid1_ready, 1)
                if 4 in live:
                    u, b = i - 4, (k - 4) % 2
                    act.wait_ge(boostT_done, u + 1)
                    act.activation(boostt[:, b].rearrange("p g t -> p (g t)"), bZ[:, 0:TG * 128], ACT.Copy).then_inc(boostT_ready, 1)
                if 3 in live:
                    b = (k - 3) % 2
                    for g in range(TG):
                        weights(w_up2[:, b, g, :], e[TG + g])
                if 4 in live:
                    u, b = i - 4, (k - 4) % 2
                    act.wait_ge(up2_done, u + 1)
                    act.activation(hid2[:, b].rearrange("p g s t -> p (g s t)"), bO[:, :], ACT.Relu).then_inc(hid2_ready, 1)
            skewed(act, UNITS, RING, [2, 3, 4], unit)

        @block.vector
        def _(dve):
            def body(i, k, live):
                if 4 in live:
                    q, b = i - 4, k % 2
                    dve.wait_ge(scale1_ready, q + 1)
                    dve.scalar_tensor_tensor(shift1[:, b, :], mv1[:, b, :, 0], -1.0, scale1[:, b, :],
                                             ALU.mult, ALU.mult).then_inc(shift1_ready, 1)
                if 2 in live:
                    q, b = i - 2, k % 2
                    dve.wait_ge(scores_done, q + 1)
                    dve.tensor_reduce(negmax[:, b, :], bL[:, :].rearrange("p (g t) -> p g t", g=G)[:, :, 0:T],
                                      AX_X, ALU.max, negate=True).then_inc(max_ready, 1)
                if 0 in live:
                    q, r = i, k
                    dve.wait_ge(x_ready[r], (q - r) * 8 + 32)
                    for g in range(G):
                        v = dve.bn_stats(stats[:, g, :], x_in[:, r, g, :])
                    v.then_inc(stats_ready, 1)
                if 5 in live:
                    q = i - 5
                    dve.wait_ge(router_done, q + 1)
                    dve.tensor_tensor(lg[:, :, :], bO[:, G * D:G * D + G * E].rearrange("p (g e) -> p g e", g=G),
                                      rb_bc[:, :, :], ALU.add).then_inc(lg_ready, 1)
                if 0 in live:
                    dve.wait_ge(stats_ready, i + 1)
                    if 3 not in live:
                        dve.nop(nofuse=True)
                if 3 in live:
                    q, b = i - 3, (k - 3) % 2
                    if 0 not in live:
                        dve.wait_ge(prob_ready, q + 1)
                    dve.reciprocal(rden[:, :], denom[:, b, :]).then_inc(rden_ready, 1)
                if 0 in live:
                    q, b = i, k % 2
                    for g in range(G):
                        v = dve.bn_aggr(mv[:, b, g, :], stats[:, g, :])
                    v.then_inc(mv_ready, 1)
                if 6 in live:
                    q = i - 6
                    dve.wait_ge(rank_done, q + 1)
                    dve.tensor_tensor(hotR[:, :, :], bR[:, 0:G * CODES].rearrange("p (g c) -> p g c", g=G),
                                      hot[:, bass.ts(q, G), :], ALU.mult).then_inc(hotR_ready, 1)
                if 0 in live:
                    q, b = i, k % 2
                    dve.wait_ge(mv_ready, q + 1)
                    dve.tensor_scalar(var_ab[:, b, 0, :], mv[:, b, :, 1], 1.0 + EPS_RMS, EPS_RMS * EPS_LN,
                                      ALU.mult, ALU.add)
                    dve.tensor_scalar(var_ab[:, b, 1, :], mv[:, b, :, 1], EPS_LN, 4.0, ALU.add, ALU.mult).then_inc(var_ready, 1)
                if 3 in live:
                    q, r, b = i - 3, (k - 3) % 4, (k - 3) % 2
                    dve.wait_ge(attended, q + 1)
                    dve.wait_ge(rden_ready, q + 1)
                    for g in range(G):
                        v = dve.scalar_tensor_tensor(diff[:, g, :], bO[:, g * D:(g + 1) * D], rden[:, g:g + 1],
                                                     h0_half[:, r, g, :], ALU.mult, ALU.subtract)
                    v.then_inc(diff_ready, 1)
                if 6 in live:
                    q, b = i - 6, k % 2
                    dve.wait_ge(hotR_ready, q + 1)
                    dve.tensor_reduce(rank[:, bass.ts(q, G)], hotR[:, :, :], AX_X, ALU.add).then_inc(rank_ready, 1)
                    dve.wait_ge(lexp_ready, q + 1)
                    dve.tensor_reduce(lsum[:, :], lexp[:, b, :, :], AX_X, ALU.add).then_inc(lsum_ready, 1)
                if 3 in live:
                    q, r, b = i - 3, (k - 3) % 4, (k - 3) % 2
                    dve.wait_ge(diff_ready, q + 1)
                    dve.scalar_tensor_tensor(gated[:, b, :, :], tanh_z[:, r, :, :], 1.0, diff[:, :, :],
                                             ALU.add, ALU.mult).then_inc(gated_ready, 1)
                if 5 in live:
                    q, b = i - 5, (k - 5) % 2
                    dve.wait_ge(lg_ready, q + 1)
                    dve.nop(nofuse=True)
                    for g in range(G):
                        v = dve.max(top[:, g, :], lg[:, g, :])
                    v.then_inc(top_ready, 1)
                if 6 in live:
                    q, r = i - 6, (k - 6) % 4
                    dve.wait_ge(lsum_ready, q + 1)
                    dve.reciprocal(rec[:, r, :, 2 * D:2 * D + 1], lsum[:, :].unsqueeze(2)).then_inc(weight1_ready, 1)
                if 5 in live:
                    q, b = i - 5, (k - 5) % 2
                    dve.wait_ge(top_ready, q + 1)
                    dve.tensor_tensor(ldiff[:, b, :, :], top[:, :, :], top[:, :, 0:1].to_broadcast([128, G, E]),
                                      ALU.subtract).then_inc(ldiff_ready, 1)
                    for g in range(G):
                        v = dve.max_index(topi[:, g, :], top[:, g, :], lg[:, g, :])
                    v.then_inc(topi_ready, 1)
                if 6 in live:
                    q, r, b = i - 6, (k - 6) % 4, k % 2
                    dve.wait_ge(weight1_ready, q + 1)
                    dve.tensor_tensor(rec[:, r, :, 2 * D + 1:2 * D + 2], rec[:, r, :, 2 * D:2 * D + 1],
                                      lexp[:, b, :, 1:2], ALU.mult).then_inc(weights_ready, 1)
                if 0 in live:
                    q, b = i, k % 2
                    dve.wait_ge(scales_ready, q + 1)
                    dve.scalar_tensor_tensor(shift[:, b, 0:2, :], mv[:, b, :, 0].unsqueeze(1).to_broadcast([128, 2, G]), -1.0,
                                             scale[:, b, 0:2, :], ALU.mult, ALU.mult).then_inc(shift_ready, 1)
                    dve.tensor_scalar(scale[:, b, 2, :], scale[:, b, 1, :], 2.0, 1.0, ALU.mult, ALU.add)
                if 5 in live:
                    q = i - 5
                    dve.wait_ge(topi_ready, q + 1)
                    dve.scalar_tensor_tensor(code[:, bass.ts(q, G)], topi[:, :, 0], float(E), topi[:, :, 1],
                                             ALU.mult, ALU.add).then_inc(code_ready, 1)
                if 0 in live:
                    q, b = i, k % 2
                    dve.wait_ge(shift_ready, q + 1)
                    dve.tensor_scalar(shift[:, b, 2, :], shift[:, b, 1, :], 2.0, None, ALU.mult).then_inc(coefficients_ready, 1)
                if 5 in live:
                    q = i - 5
                    dve.wait_ge(code_ready, q + 1)
                    dve.tensor_tensor(hot[:, bass.ts(q, G), :], codes_f[:, 0:CODES].unsqueeze(1).to_broadcast([128, G, CODES]),
                                      code[:, bass.ts(q, G)].unsqueeze(2).to_broadcast([128, G, CODES]),
                                      ALU.is_equal).then_inc(hot_ready, 1)
                if 3 in live:
                    q, b = i - 3, (k - 3) % 2
                    dve.wait_ge(x1_ready, q + 1)
                    for g in range(G):
                        v = dve.bn_stats(stats1[:, g, :], x1[:, b, g, :])
                    v.then_inc(stats1_ready, 1)
                    dve.wait_ge(stats1_ready, q + 1)
                    dve.nop(nofuse=True)
                    for g in range(G):
                        v = dve.bn_aggr(mv1[:, b, g, :], stats1[:, g, :])
                    v.then_inc(mv1_ready, 1)
                    dve.wait_ge(mv1_ready, q + 1)
                    dve.tensor_scalar(var1[:, b, :], mv1[:, b, :, 1], EPS_LN, None, ALU.add).then_inc(var1_ready, 1)
                if isinstance(i, int) and i == 0:
                    split_biases()

            def split_biases():
                dve.wait_ge(s_bias, 48)
                dve.tensor_scalar(bias_col[:, 24:25], bias_col[:, 24:25], 0.5, None, ALU.mult).then_inc(vs, 1)
                dve.wait_ge(vs, 1)
                dve.tensor_copy(part0[:, 0, :], bias_col[:, :]).then_inc(vs, 1)
                dve.wait_ge(vs, 2)
                dve.tensor_tensor(rest1[:, :], bias_col[:, :], part0[:, 0, :], ALU.subtract).then_inc(vs, 1)
                dve.wait_ge(vs, 3)
                dve.tensor_copy(part0[:, 1, :], rest1[:, :]).then_inc(vs, 1)
                dve.wait_ge(vs, 4)
                dve.tensor_tensor(rest2[:, :], rest1[:, :], part0[:, 1, :], ALU.subtract).then_inc(vs, 1)
                dve.wait_ge(vs, 5)
                dve.tensor_copy(part0[:, 2, :], rest2[:, :]).then_inc(V_part, 1)

            skewed(dve, NP, UNROLL, [0, 2, 3, 4, 5, 6], body)

            dve.wait_ge(rank_base_done, NP)
            dve.wait_ge(s_c, 3)
            dve.wait_ge(rank_ready, NP)
            dve.tensor_scalar(count_i[:, :], bR[:, 0:CODES], 127.0, None, ALU.add)
            dve.tensor_copy(rank_i[:, :], rank[:, :])
            dve.tensor_copy(token_f[:, :], token_i[:, :])
            dve.tensor_copy(part_f[:, :], part_i[:, :]).then_inc(vb, 1)
            dve.wait_ge(vb, 1)
            dve.tensor_scalar(tiles_i[:, :], count_i[:, :], 7, None, ALU.logical_shift_right)
            dve.tensor_scalar(rank_hi[:, :], rank_i[:, :], 7, None, ALU.logical_shift_right)
            dve.tensor_scalar(rank_lo[:, :], rank_i[:, :], 127, None, ALU.bitwise_and).then_inc(vb, 1)
            dve.wait_ge(vb, 2)
            dve.tensor_copy(tiles_f[:, :], tiles_i[:, :])
            dve.tensor_copy(place[:, :], rank_lo[:, :]).then_inc(vb, 1)
            dve.wait_ge(vb, 3)
            dve.tensor_tensor_scan(tile_end[:, :], ones_f[:, :], tiles_f[:, :], 0.0, ALU.mult, ALU.add).then_inc(vb, 1)
            dve.wait_ge(vb, 4)
            dve.tensor_tensor(start_h[:, :], tile_end[:, :], tiles_f[:, :], ALU.subtract)
            dve.tensor_scalar(ended[:, :], tile_end[:, :], part_f[:, 0:1], None, ALU.is_le).then_inc(vb, 1)
            dve.wait_ge(vb, 5)
            dve.tensor_reduce(tile_code[:, :], ended[:, :], AX_X, ALU.add).then_inc(vb, 1)
            dve.tensor_tensor(hot_start[:, :, :], hot[:, :, :],
                              start_h[:, :].unsqueeze(1).to_broadcast([128, 64, CODES]), ALU.mult).then_inc(vb, 1)
            dve.wait_ge(vb, 7)
            dve.tensor_scalar(tile_code[:, :], tile_code[:, :], float(CODES - 1), None, ALU.min).then_inc(B_col, 1)
            dve.tensor_reduce(start_of[:, :], hot_start[:, :, :], AX_X, ALU.add).then_inc(vb, 1)
            dve.wait_ge(vb, 8)
            dve.tensor_tensor(tile_of[:, :], start_of[:, :], rank_hi[:, :], ALU.add).then_inc(vb, 1)
            dve.wait_ge(vb, 9)

            def batch(i, k):
                free(dve, B_free, 1, i, 4)
                dve.tensor_scalar(is_place[:, k, :], codes_f[:, :], place[:, bass.ds(i, 1)], None, ALU.is_equal)
                dve.tensor_scalar(is_tile[:, k, :], codes_f[:, 0:TILES], tile_of[:, bass.ds(i, 1)],
                                  token_f[:, bass.ds(i, 1)], ALU.is_equal, ALU.mult).then_inc(B_place, 1)
            for i in range(4):
                batch(i, i)
            with dve.Fori(1, B // 4) as turn:
                for k in range(4):
                    batch(turn * 4 + k, k)

            dve.wait_ge(B_free, B)
            dve.tensor_scalar(empty[:, :], bO[:, 0:TILES], 0.5, SKIPPED, ALU.is_lt, ALU.mult)
            dve.tensor_scalar(gather_at[:, :], bO[:, 0:TILES], -1.0, 0.0, ALU.add, ALU.max)
            dve.tensor_copy(slots[:, :], bO[:, 0:TILES]).then_inc(vb, 1)
            dve.wait_ge(vb, 10)
            dve.scalar_tensor_tensor(scatter_at[:, :], slots[:, :], -1.0, empty[:, :], ALU.add, ALU.add).then_inc(B_idx, 1)
            dve.wait_ge(B_row, 1)
            dve.tensor_copy(tile_row[:, :], bP[0:1, 0:128]).then_inc(vb, 1)
            dve.wait_ge(vb, 11)
            for n, lag, op, by in ((0, 3, ALU.logical_shift_right, 3), (1, 4, ALU.bitwise_and, E - 1),
                                   (2, 4, ALU.logical_shift_right, 3), (3, 5, ALU.bitwise_and, E - 1)):
                v = dve.tensor_scalar(plan[:, lag:lag + UNITS, n, :],
                                      tile_row[:, 0:TILES].rearrange("p (u g) -> p u g", g=TG), by, None, op)
            v.then_inc(B_rowdone, 1)

            dve.wait_ge(B_idx, 1)

            def unit(i, k, live):
                if 0 in live:
                    u, r = i, k
                    if k % 2 == 0:
                        free(dve, records_transposed, 1, u, RING - 1)
                        dve.tensor_copy(gather_now[:, r * TG:(r + 2) * TG],
                                        gather_at[:, bass.ds(u * TG, 2 * TG)]).then_inc(gather_cols, 2)
                if 4 in live:
                    u, r, b = i - 4, (k - 4) % RING, (k - 4) % 2
                    dve.wait_ge(out1_done, u + 1)
                    for g in range(TG):
                        dve.scalar_tensor_tensor(mixed[:, b, g, :], bP[:, g * D:(g + 1) * D], tok[:, r, g, 2 * D:2 * D + 1],
                                                 tok[:, r, g, 0:D], ALU.mult, ALU.add)
                    dve.scalar_tensor_tensor(boost[:, b], bP[:, 0:TG * D].rearrange("p (g d) -> p g d", g=TG), 0.5,
                                             tok[:, r, :, 0:D], ALU.mult, ALU.add).then_inc(boost_ready, 1)
                if 6 in live:
                    u, r, b, o = i - 6, (k - 6) % RING, k % 2, (k - 6) % ROWS
                    if r % 2 == 0:
                        dve.tensor_copy(scatter_now[:, r * TG:(r + 2) * TG],
                                        scatter_at[:, bass.ds(u * TG, 2 * TG)]).then_inc(scatter_cols, 1)
                    dve.wait_ge(scalez_ready, u + 1)
                    for g in range(TG):
                        v = dve.scalar_tensor_tensor(y[:, g, :], z[:, b, g, :], mvz[:, b, g, 0:1], gamma_bc[:, :],
                                                     ALU.subtract, ALU.mult)
                    v.then_inc(y_ready, 1)
                    dve.wait_ge(y_ready, u + 1)
                    for g in range(TG):
                        if not (isinstance(u, int) and u < ROWS):
                            dve.wait_ge(scattered[o * TG + g], (u - o) * (16 // ROWS))
                        v = dve.scalar_tensor_tensor(row_out[:, o, g, :], y[:, g, :], scalez[:, b, g:g + 1], tok[:, r, g, D:2 * D],
                                                     ALU.mult, ALU.add)
                    v.then_inc(rows_ready, 1)
                if 5 in live:
                    u, r, b = i - 5, (k - 5) % RING, (k - 5) % 2
                    dve.wait_ge(out2_done, u + 1)
                    for g in range(TG):
                        dve.scalar_tensor_tensor(z[:, b, g, :], bR[:, g * D:(g + 1) * D], tok[:, r, g, 2 * D + 1:2 * D + 2],
                                                 mixed[:, b, g, :], ALU.mult, ALU.add).then_inc(z_ready, 1)
                    for g in range(TG):
                        dve.wait_ge(z_ready, TG * u + g + 1)
                        dve.bn_stats(statsz[:, b, g, :], z[:, b, g, :]).then_inc(zstats_ready, 1)
                    dve.wait_ge(zstats_ready, TG * (u + 1))
                    dve.nop(nofuse=True)
                    for g in range(TG):
                        v = dve.bn_aggr(mvz[:, b, g, :], statsz[:, b, g, :])
                    v.then_inc(zmv_ready, 1)
                    dve.wait_ge(zmv_ready, u + 1)
                    dve.tensor_scalar(varz[:, b, :], mvz[:, b, :, 1], EPS_LN, None, ALU.add).then_inc(varz_ready, 1)
            skewed(dve, UNITS, RING, [0, 4, 5, 6], unit)
            dve.wait_ge(scatter_cols, UNITS // 2)


_INS = ["x", "ctx_1024", "L0_xattn_q_w", "L0_xattn_k_w", "L0_xattn_norm_w", "L0_xattn_gate_w", "L0_xattn_gate_b",
        "L0_ffn_gate_W", "L0_ffn_gate_b", "L0_ffn_W1", "L0_ffn_b1", "L0_ffn_W2", "L0_ffn_b2", "L0_ffn_ln_gamma",
        "L0_ffn_ln_beta"]
_OUTS = [((B, S, D), "float32")]


def kernel(**inputs):
    import numpy as np
    import concourse.bacc as bacc
    from concourse.bass_utils import run_bass_kernel_spmd

    nc = bacc.Bacc("TRN2", target_bir_lowering=False, num_devices=1)
    arrays, args = {}, []
    for name in _INS:
        a = np.ascontiguousarray(inputs[name])
        arrays[f"in_{name}_dram"] = a
        args.append(nc.dram_tensor(f"in_{name}_dram", a.shape, mybir.dt.from_np(a.dtype), kind="ExternalInput").ap())
    for n, (shape, dtype) in enumerate(_OUTS):
        args.append(nc.dram_tensor(f"out_{n}_dram", shape, mybir.dt.from_np(np.dtype(dtype)), kind="ExternalOutput").ap())
    program(nc, *args)
    r = run_bass_kernel_spmd(nc, [arrays], core_ids=[0])
    return r.results[0]["out_0_dram"]
```

```python
from contextlib import ExitStack

import concourse.bass as bass
from concourse import mybir

F32 = mybir.dt.float32
BF16 = mybir.dt.bfloat16
U32 = mybir.dt.uint32
I32 = mybir.dt.int32
ALU = mybir.AluOpType
ACT = mybir.ActivationFunctionType
AX_X = mybir.AxisListType.X

B, S, D = 64, 128, 128
SC = 77
E, H = 8, 256
HH = H // 128
G = 2
NP = B // G
CODES = E * E
TILES = 120
T = S + SC
REC = 2 * D + 2
BC = E * D // 128 + 1
EPS_LN, EPS_RMS = 1e-5, 1e-6
NEG = -1.0e30
UNROLL = 4
TG = 2
UNITS = TILES // TG
BG = 4
PD = 4
RING = 8
ROWS = 4
SKIPPED = 1.0e6
UP = H + HH
WE = UP + HH * D


def skewed(engine, count, unroll, lags, body):
    last = max(lags)
    first = -(-last // unroll) * unroll
    for i in range(first):
        body(i, i % unroll, [l for l in lags if i >= l])
    end = first + (count - first) // unroll * unroll
    with engine.Fori(first // unroll, end // unroll) as turn:
        for k in range(unroll):
            body(turn * unroll + k, k, lags)
    for i in range(end, count + last):
        body(i, i % unroll, [l for l in lags if 0 <= i - l < count])


def free(engine, semaphore, per, unit, depth):
    if isinstance(unit, int) and unit < depth:
        return
    engine.wait_ge(semaphore, (unit - (depth - 1)) * per)


def program(nc, x, ctx, q_w, k_w, norm_w, gate_w, gate_b, router_w, router_b, W1, b1, W2, b2,
            gamma, beta, out):
    stack = ExitStack()
    with stack:
        def sb(name, shape, dt=F32):
            return stack.enter_context(nc.sbuf_tensor(name, shape, dt))

        def sem(name):
            return stack.enter_context(nc.semaphore(name))

        out_rows = out.rearrange("b s d -> (b s) d")
        records = nc.dram_tensor("records", [B * S, REC], F32).ap()

        ident = sb("ident", [128, 128])
        ident_h = sb("ident_h", [128, 128], BF16)
        mask_h = sb("mask_h", [128, 128], BF16)
        before_h = sb("before_h", [128, 128], BF16)
        rest_h = sb("rest_h", [128, 128], BF16)
        ones_h = sb("ones_h", [128, 128], BF16)
        zeros_h = sb("zeros_h", [128, 128], BF16)
        codes_i = sb("codes_i", [128, 128], I32)
        codes_f = sb("codes_f", [128, 128])
        minus_half = sb("minus_half", [128, 2 * G])
        qw = sb("qw", [128, D])
        kw = sb("kw", [128, D])
        gw = sb("gw", [128, D])
        score_m = sb("score_m", [128, D])
        gwT = sb("gwT", [128, D])
        w_bc = sb("w_bc", [128, G, D])
        beta_bc = sb("beta_bc", [128, G, D])
        gamma_bc = sb("gamma_bc", [128, D])
        rw = sb("rw", [128, E])
        rb_bc = sb("rb_bc", [128, G, E])
        We = sb("We", [128, E, WE])
        x_in = sb("x_in", [128, 4, G, D])
        c_in = sb("c_in", [SC, 4, G, D])
        stats = sb("stats", [128, G, 6])
        mv = sb("mv", [128, 2, G, 2])
        var_ab = sb("var_ab", [128, 2, 2, G])
        scale = sb("scale", [128, 2, 2, G])
        shift = sb("shift", [128, 2, 2, G])
        normed = sb("normed", [128, 2, G, D])
        h0_half = sb("h0_half", [128, 4, G, D])
        vw = sb("vw", [128, 4, G, D])
        xh = sb("xh", [128, 4, G, D])
        tT = sb("tT", [128, 2, 2, G, D])
        cA = sb("cA", [128, 2, G * SC + G * S])
        tanh_z = sb("tanh_z", [128, 4, G, D])
        negmax = sb("negmax", [128, 2, G])
        prob = sb("prob", [128, 2, G, T])
        denom = sb("denom", [128, 2, G])
        rden = sb("rden", [128, G])
        pTs = sb("pTs", [128, 2, G, S])
        pTc = sb("pTc", [SC, 2, G, S])
        diff = sb("diff", [128, G, D])
        gated = sb("gated", [128, 2, G, D])
        x1 = sb("x1", [128, 2, G, D])
        stats1 = sb("stats1", [128, G, 6])
        mv1 = sb("mv1", [128, 2, G, 2])
        var1 = sb("var1", [128, 2, G])
        scale1 = sb("scale1", [128, 2, G])
        shift1 = sb("shift1", [128, 2, G])
        rec = sb("rec", [128, 4, G, REC])
        h1T = sb("h1T", [128, 2, G, S])
        lg = sb("lg", [128, G, E])
        top = sb("top", [128, G, E])
        topi = sb("topi", [128, G, E], U32)
        ldiff = sb("ldiff", [128, 2, G, E])
        lexp = sb("lexp", [128, 2, G, E])
        lsum = sb("lsum", [128, G])
        code = sb("code", [128, 64])
        hot = sb("hot", [128, 64, CODES], BF16)
        hotR = sb("hotR", [128, G, CODES])
        rank = sb("rank", [128, 64])

        bias_col = sb("bias_col", [128, BC])
        bias_parts = sb("bias_parts", [128, 3, BC], BF16)
        rest1 = sb("rest1", [128, BC])
        rest2 = sb("rest2", [128, BC])
        b2s = sb("b2s", [3, E, D], BF16)
        gbs = sb("gbs", [3, D], BF16)
        count_i = sb("count_i", [128, CODES], I32)
        tiles_i = sb("tiles_i", [128, CODES], I32)
        tiles_f = sb("tiles_f", [128, CODES])
        tile_end = sb("tile_end", [128, CODES])
        ones_f = sb("ones_f", [128, CODES])
        start_h = sb("start_h", [128, CODES], BF16)
        hot_start = sb("hot_start", [128, 64, CODES], BF16)
        half1 = sb("half1", [128, 64, CODES // 2], BF16)
        half2 = sb("half2", [128, 64, CODES // 4], BF16)
        half3 = sb("half3", [128, 64, CODES // 8], BF16)
        start_of = sb("start_of", [128, 64])
        rank_i = sb("rank_i", [128, 64], I32)
        rank_hi = sb("rank_hi", [128, 64], I32)
        rank_lo = sb("rank_lo", [128, 64], I32)
        tile_of = sb("tile_of", [128, 64])
        place = sb("place", [128, 64])
        token_i = sb("token_i", [128, 64], I32)
        token_f = sb("token_f", [128, 64])
        part_i = sb("part_i", [128, 1], I32)
        part_f = sb("part_f", [128, 1])
        is_place = sb("is_place", [128, PD, BG, 128])
        distance = sb("distance", [128, PD, BG - 1, 128])
        is_tile = sb("is_tile", [128, PD, BG, TILES])
        ended = sb("ended", [128, CODES])
        tile_code = sb("tile_code", [128, 1])
        tile_row = sb("tile_row", [1, 128], I32)
        plan = sb("plan", [1, UNITS + 8, 4, TG], I32)
        slots = sb("slots", [128, TILES])
        empty = sb("empty", [128, TILES])
        gather_at = sb("gather_at", [128, TILES], U32)
        scatter_at = sb("scatter_at", [128, TILES], U32)
        gather_now = sb("gather_now", [128, RING * TG], U32)
        scatter_now = sb("scatter_now", [128, RING * TG], U32)
        tok = sb("tok", [128, RING, TG, REC])
        w_up1 = sb("w_up1", [128, 2, TG, UP])
        w_up2 = sb("w_up2", [128, 2, TG, UP])
        h1t = sb("h1t", [128, 2, TG, 128])
        hid1 = sb("hid1", [128, 2, TG, HH, 128])
        boost = sb("boost", [128, 2, TG, D])
        mixed = sb("mixed", [128, 2, TG, D])
        boostt = sb("boostt", [128, 2, TG, 128])
        hid2 = sb("hid2", [128, 2, TG, HH, 128])
        z = sb("z", [128, 2, TG, D])
        statsz = sb("statsz", [128, 2, TG, 6])
        mvz = sb("mvz", [128, 2, TG, 2])
        varz = sb("varz", [128, 2, TG])
        scalez = sb("scalez", [128, 2, TG])
        y = sb("y", [128, TG, D])
        row_out = sb("row_out", [128, ROWS, TG, D])

        def bank(name):
            return stack.enter_context(nc.psum_tensor(name, [128, 512], F32))

        bT, bC, bL, bP, bZ, bO, bH, bR = [bank(f"bank{n}") for n in range(8)]

        rows_in, biases_in, norm_weight_in = sem("rows_in"), sem("biases_in"), sem("norm_weight_in")
        attention_weights_in, experts_in = sem("attention_weights_in"), sem("experts_in")
        constants_ready, setup_products_done = sem("constants_ready"), sem("setup_products_done")
        setup_weights_ready, bias_step_done = sem("setup_weights_ready"), sem("bias_step_done")
        bias_parts_ready, bias_parts_out = sem("bias_parts_ready"), sem("bias_parts_out")
        bias_parts_in = sem("bias_parts_in")
        lg_ready, weight1_ready, stats_ready = sem("lg_ready"), sem("weight1_ready"), sem("stats_ready")
        mv_ready, var_ready, scales_ready = sem("mv_ready"), sem("var_ready"), sem("scales_ready")
        shift_ready, xh_ready, tokens_normed = sem("shift_ready"), sem("xh_ready"), sem("tokens_normed")
        vw_ready, tokens_transposed, tT_ready = sem("vw_ready"), sem("tokens_transposed"), sem("tT_ready")
        scoremix_done, gate_done, cA_ready = sem("scoremix_done"), sem("gate_done"), sem("cA_ready")
        tanh_ready, scores_done, max_ready = sem("tanh_ready"), sem("scores_done"), sem("max_ready")
        prob_ready, prob_transposed, pT_ready = sem("prob_ready"), sem("prob_transposed"), sem("pT_ready")
        attended, rden_ready, diff_ready = sem("attended"), sem("rden_ready"), sem("diff_ready")
        gated_ready, x1_ready, stats1_ready = sem("gated_ready"), sem("x1_ready"), sem("stats1_ready")
        mv1_ready, var1_ready, scale1_ready = sem("mv1_ready"), sem("var1_ready"), sem("scale1_ready")
        shift1_ready, h1_ready, x1b_ready = sem("shift1_ready"), sem("h1_ready"), sem("x1b_ready")
        h1_transposed, h1T_ready, router_done = sem("h1_transposed"), sem("h1T_ready"), sem("router_done")
        top_ready, topi_ready, ldiff_ready = sem("top_ready"), sem("topi_ready"), sem("ldiff_ready")
        lexp_ready, code_ready, hot_ready = sem("lexp_ready"), sem("code_ready"), sem("hot_ready")
        rank_done, hotR_ready, rank_ready = sem("rank_done"), sem("hotR_ready"), sem("rank_ready")
        rank_base_done, lsum_ready, weights_ready = sem("rank_base_done"), sem("lsum_ready"), sem("weights_ready")
        x_ready = [sem(f"x_ready{k}") for k in range(4)]
        stored = [sem(f"record_stored{k}") for k in range(4)]
        counts_ready, tiles_ready, tiles_f_ready = sem("counts_ready"), sem("tiles_ready"), sem("tiles_f_ready")
        tile_end_ready, starts_ready, ended_ready = sem("tile_end_ready"), sem("starts_ready"), sem("ended_ready")
        hot_start_ready, tile_code_ready = sem("hot_start_ready"), sem("tile_code_ready")
        start_of_ready, tile_of_ready, slots_ready = sem("start_of_ready"), sem("tile_of_ready"), sem("slots_ready")
        tile_row_ready, tile_hot_ready, hots_used = sem("tile_row_ready"), sem("tile_hot_ready"), sem("hots_used")
        place_hot_ready, places_ready = sem("place_hot_ready"), sem("places_ready")
        distance_ready, tile_codes_final = sem("distance_ready"), sem("tile_codes_final")
        tile_row_done, plan_ready = sem("tile_row_done"), sem("plan_ready")
        slot_tables_ready = sem("slot_tables_ready")
        gather_cols, scatter_cols = sem("gather_cols"), sem("scatter_cols")
        records_transposed, recordsT_ready = sem("records_transposed"), sem("recordsT_ready")
        up1_done, hid1_ready, out1_done = sem("up1_done"), sem("hid1_ready"), sem("out1_done")
        boost_ready, mixed_ready, boostT_done = sem("boost_ready"), sem("mixed_ready"), sem("boostT_done")
        boostT_ready, up2_done, hid2_ready = sem("boostT_ready"), sem("up2_done"), sem("hid2_ready")
        out2_done, z_ready, zstats_ready = sem("out2_done"), sem("z_ready"), sem("zstats_ready")
        zmv_ready, varz_ready, scalez_ready = sem("zmv_ready"), sem("varz_ready"), sem("scalez_ready")
        y_ready, rows_ready = sem("y_ready"), sem("rows_ready")
        gathered = [sem(f"gathered{n}") for n in range(RING * TG)]
        scattered = [sem(f"scattered{n}") for n in range(ROWS * TG)]

        block = stack.enter_context(nc.Block())

        x_v = x.rearrange("(n g) s d -> n s g d", g=G)
        c_v = ctx.rearrange("(n g) s d -> n s g d", g=G)
        rec_v = records.rearrange("(n g s) r -> n s g r", g=G, s=S)
        SETUP_LOADS = 2 * G + 2
        bias_parts_dram = nc.dram_tensor("bias_parts_dram", [3, 128 * BC], BF16).ap()
        BIAS = ((0, E * D // 128), (E * D // 128, 1))

        @block.sync
        def _(sp):
            def load(i, k):
                if not (isinstance(i, int) and i < 4):
                    sp.wait_ge(xh_ready, i - 3)
                    sp.wait_ge(attended, i - 3)
                sp.dma_start(x_in[:, k, :, :], x_v[i]).then_inc(x_ready[k], 16)
                sp.dma_start(c_in[:, k, :, :], c_v[i]).then_inc(x_ready[k], 16)

            load(0, 0)
            for (at, n), src in zip(BIAS, (b2.rearrange("e (a f) -> (e a) f", f=8), gate_b.rearrange("(p a) -> p a", a=1))):
                sp.dma_start(bias_col[:, at:at + n], src).then_inc(biases_in, 16)
            row = lambda v: v.rearrange("(a n) -> a n", a=1).to_broadcast([128, v.shape[0]])
            for g in range(G):
                sp.dma_start(w_bc[:, g, :], row(norm_w)).then_inc(norm_weight_in, 16)
            load(1, 1)
            for g in range(G):
                sp.dma_start(rb_bc[:, g, :], row(router_b)).then_inc(rows_in, 16)
                sp.dma_start(beta_bc[:, g, :], row(beta)).then_inc(rows_in, 16)
            sp.dma_start(rw[:, :], router_w).then_inc(rows_in, 16)
            sp.dma_start(gamma_bc[:, :], row(gamma)).then_inc(rows_in, 16)
            sp.wait_ge(bias_parts_ready, 1)
            for at, n in BIAS[::-1]:
                sp.dma_start(bias_parts_dram[:, 128 * at:128 * (at + n)].rearrange("t (p f) -> p t f", f=n),
                             bias_parts[:, :, at:at + n], allow_slow_non_contiguous=n == 1).then_inc(bias_parts_out, 16)
            sp.wait_ge(bias_parts_out, 32)
            for (at, n), dst in zip(BIAS, (b2s[:, :, :].rearrange("t e d -> t (e d)"), gbs[:, :])):
                sp.dma_start(dst, bias_parts_dram[:, 128 * at:128 * (at + n)]).then_inc(bias_parts_in, 16)

            def body(i, k, live):
                if isinstance(i, int) and i == 4:
                    for e in range(E):
                        sp.dma_start(We[:, e, 0:H], W1[e]).then_inc(experts_in, 16)
                        sp.dma_start(We[:, e, UP:WE].rearrange("p (s d) -> p s d", s=HH),
                                     W2[e].rearrange("(s p) d -> p s d", p=128)).then_inc(experts_in, 16)
                        sp.dma_start(We[:, e, H:UP], b1[e].rearrange("(s p) -> p s", p=128),
                                     allow_slow_non_contiguous=True).then_inc(experts_in, 16)
                if 0 in live and not (isinstance(i, int) and i < 2):
                    load(i, k)
                if 7 in live:
                    q, r = i - 7, (k - 7) % 4
                    sp.wait_ge(h1_ready, q + 1)
                    sp.wait_ge(x1b_ready, q + 1)
                    sp.wait_ge(weights_ready, q + 1)
                    sp.dma_start(rec_v[q], rec[:, r, :, :]).then_inc(stored[r], 16)
            skewed(sp, NP, UNROLL, [0, 7], body)
            for r in range(4):
                sp.wait_ge(stored[r], 16 * (NP // 4))

        @block.gpsimd
        def _(pool):
            pool.memset(ident[:, :], 0.0)
            pool.memset(ident_h[:, :], 0.0)
            pool.memset(mask_h[:, :], 0.0)
            pool.memset(before_h[:, :], 0.0)
            pool.memset(rest_h[:, :], 0.0)
            pool.memset(ones_h[:, :], 1.0)
            pool.memset(zeros_h[:, :], 0.0)
            pool.memset(minus_half[:, :], -0.5)
            pool.iota(codes_i[:, :], [[1, 128]], base=0, channel_multiplier=0).then_inc(constants_ready, 1)
            pool.wait_ge(constants_ready, 1)
            for m in (ident, ident_h):
                pool.affine_select(out=m[:, :], in_=m[:, :], compare_op=ALU.not_equal, fill=1.0, base=0,
                                   pattern=[[-1, 128]], channel_multiplier=1)
            pool.affine_select(out=mask_h[:, :], in_=mask_h[:, :], compare_op=ALU.is_ge, fill=NEG, base=0,
                               pattern=[[-1, 128]], channel_multiplier=1)
            pool.affine_select(out=before_h[:, :], in_=before_h[:, :], compare_op=ALU.is_ge, fill=1.0, base=0,
                               pattern=[[-1, 128]], channel_multiplier=1)
            pool.affine_select(out=rest_h[:, :], in_=rest_h[:, :], compare_op=ALU.is_gt, fill=1.0, base=0,
                               pattern=[[1, 128]], channel_multiplier=-1)
            pool.tensor_copy(codes_f[:, :], codes_i[:, :]).then_inc(constants_ready, 1)
            pool.iota(token_i[:, :], [[S, B]], base=1, channel_multiplier=1)
            pool.iota(part_i[:, :], [[0, 1]], base=0, channel_multiplier=1)
            pool.memset(plan[:, :, :, :], 0)
            pool.memset(ones_f[:, :], 1.0).then_inc(constants_ready, 1)

            def body(i, k, live):
                if 1 in live:
                    q, r, b = i - 1, (k - 1) % 4, (k - 1) % 2
                    if isinstance(q, int) and q == 0:
                        pool.wait_ge(norm_weight_in, 16 * G)
                    pool.wait_ge(tokens_normed, q + 1)
                    pool.tensor_tensor(vw[:, r, :, :], normed[:, b, :, :], w_bc[:, :, :], ALU.mult).then_inc(vw_ready, 1)
                if 0 in live:
                    q, b = i, k % 2
                    pool.wait_ge(var_ready, q + 1)
                    pool.tensor_tensor(scale[:, b].rearrange("p a g -> p (a g)"),
                                       var_ab[:, b].rearrange("p a g -> p (a g)"),
                                       minus_half[:, :], ALU.pow).then_inc(scales_ready, 1)
                if 3 in live:
                    q, r, b = i - 3, (k - 3) % 4, (k - 3) % 2
                    pool.wait_ge(gated_ready, q + 1)
                    pool.tensor_tensor(x1[:, b, :, :], gated[:, b, :, :], xh[:, r, :, :], ALU.add).then_inc(x1_ready, 1)
                    if isinstance(q, int) and q == 0:
                        pool.wait_ge(rows_in, 16 * SETUP_LOADS)
                    pool.wait_ge(x1_ready, q + 1)
                    if not (isinstance(q, int) and q < 4):
                        pool.wait_ge(stored[r], (q - r) * 4)
                    pool.tensor_tensor(rec[:, r, :, D:2 * D], x1[:, b, :, :], beta_bc[:, :, :], ALU.add).then_inc(x1b_ready, 1)
                    pool.wait_ge(var1_ready, q + 1)
                    pool.tensor_tensor(scale1[:, b, :], var1[:, b, :], minus_half[:, 0:G], ALU.pow).then_inc(scale1_ready, 1)
            skewed(pool, NP, UNROLL, [0, 1, 3], body)

            pool.wait_ge(slot_tables_ready, 1)
            for r in range(4):
                pool.wait_ge(stored[r], 16 * (NP // 4))

            def unit(i, k, live):
                if 1 in live:
                    u, r = i - 1, (k - 1) % RING
                    pool.wait_ge(gather_cols, u + 1)
                    free(pool, rows_ready, 1, u, RING)
                    pool.nop(nofuse=True)
                    for g in range(TG):
                        n = r * TG + g
                        pool.indirect_dma_start(tok[:, r, g, :], None, records,
                                                bass.IndirectOffsetOnAxis(ap=gather_now[:, n:n + 1], axis=0)
                                                ).then_inc(gathered[n], 16)
                if 6 in live:
                    u, b = i - 6, k % 2
                    pool.wait_ge(varz_ready, u + 1)
                    pool.tensor_tensor(scalez[:, b, :], varz[:, b, :], minus_half[:, 0:TG], ALU.pow).then_inc(scalez_ready, 1)
                if 7 in live:
                    u, b = i - 7, (k - 7) % ROWS
                    pool.wait_ge(rows_ready, u + 1)
                    pool.nop(nofuse=True)
                    for g in range(TG):
                        n = (k - 7) % RING * TG + g
                        pool.indirect_dma_start(out_rows, bass.IndirectOffsetOnAxis(ap=scatter_now[:, n:n + 1], axis=0),
                                                row_out[:, b, g, :], None, bounds_check=B * S - 1, oob_is_err=False
                                                ).then_inc(scattered[b * TG + g], 16)
            skewed(pool, UNITS, RING, [1, 6, 7], unit)
            for n in range(ROWS * TG):
                pool.wait_ge(scattered[n], 16 * (UNITS // ROWS))

        @block.tensor
        def _(pe):
            pe.wait_ge(constants_ready, 2)
            pe.matmul(bR[:, 0:G * CODES], ones_h[:, :], zeros_h[:, :], start=True, stop=False, skip_group_check=True)
            pe.wait_ge(attention_weights_in, 48)
            pe.matmul(bL[:, 0:128], qw[:, :], kw[:, :], start=True, stop=True)
            pe.transpose(bL[:, 128:256], gw[:, :], ident[:, :]).then_inc(setup_products_done, 1)

            def body(i, k, live):
                first = isinstance(i, int)
                if 1 in live:
                    q, r = i - 1, (k - 1) % 4
                    pe.wait_ge(x_ready[r], (q - r) * 8 + 32)
                    for g in range(G):
                        pe.transpose(bC[:, g * SC:(g + 1) * SC], c_in[:, r, g, :], ident[0:SC, 0:SC])
                    pe.wait_ge(tokens_normed, q + 1)
                    for g in range(G):
                        pe.transpose(bT[:, (G + g) * S:(G + g + 1) * S], h0_half[:, r, g, :], ident[:, :])
                    pe.wait_ge(vw_ready, q + 1)
                    for g in range(G):
                        mm = pe.transpose(bT[:, g * S:(g + 1) * S], vw[:, r, g, :], ident[:, :])
                    mm.then_inc(tokens_transposed, 1)
                if 2 in live:
                    q, b = i - 2, k % 2
                    if first and q == 0:
                        pe.wait_ge(bias_parts_in, 32)
                    for g in range(G):
                        pe.matmul(bZ[:, g * D:(g + 1) * D], tT[:, b, 1, g, :], gwT[:, :], start=True, stop=False)
                        mm = pe.matmul(bZ[:, g * D:(g + 1) * D], ones_h[0:3, :], gbs[:, :], start=False, stop=True)
                    mm.then_inc(gate_done, 1)
                if 4 in live:
                    q, r = i - 4, k % 4
                    pe.wait_ge(h1_ready, q + 1)
                    for g in range(G):
                        mm = pe.transpose(bH[:, g * S:(g + 1) * S], rec[:, r, g, 0:D], ident[:, :])
                    mm.then_inc(h1_transposed, 1)
                if 1 in live:
                    q, b = i - 1, (k - 1) % 2
                    if first and q == 0:
                        pe.wait_ge(setup_weights_ready, 1)
                    pe.wait_ge(tT_ready, q + 1)
                    pe.matmul(bC[:, G * SC:G * SC + G * S], score_m[:, :],
                              tT[:, b, 0, :, :].rearrange("p g s -> p (g s)"), start=True, stop=True).then_inc(scoremix_done, 1)
                if 2 in live:
                    q, b = i - 2, k % 2
                    pe.wait_ge(prob_ready, q + 1)
                    for g in range(G):
                        pe.transpose(bP[:, g * S:(g + 1) * S], prob[:, b, g, 0:S], ident[:, :])
                        mm = pe.transpose(bP[0:SC, (G + g) * S:(G + g + 1) * S], prob[:, b, g, S:T], ident[:, :])
                    mm.then_inc(prob_transposed, 1)
                if 1 in live:
                    q, b = i - 1, (k - 1) % 2
                    pe.wait_ge(cA_ready, q + 1)
                    for g in range(G):
                        A = cA[:, b, G * SC + g * S:G * SC + (g + 1) * S]
                        o = g * 256
                        pe.matmul(bL[:, o:o + S], A, tT[:, b, 0, g, :], start=True, stop=False)
                        pe.matmul(bL[:, o:o + S], ident_h[:, :], mask_h[:, :], start=False, stop=True)
                        mm = pe.matmul(bL[:, o + S:o + T], A, cA[:, b, g * SC:(g + 1) * SC], start=True, stop=True)
                    mm.then_inc(scores_done, 1)
                if 2 in live:
                    q, r, b = i - 2, (k - 2) % 4, k % 2
                    free(pe, diff_ready, 1, q, 1)
                    pe.wait_ge(pT_ready, q + 1)
                    for g in range(G):
                        pe.matmul(bO[:, g * D:(g + 1) * D], pTs[:, b, g, :], vw[:, r, g, :], start=True, stop=False)
                        mm = pe.matmul(bO[:, g * D:(g + 1) * D], pTc[:, b, g, :], c_in[:, r, g, :], start=False, stop=True)
                    mm.then_inc(attended, 1)
                if 6 in live:
                    q = i - 6
                    pe.wait_ge(hotR_ready, q + 1)
                    pair_hot = hot[:, bass.ts(q, G), :].rearrange("p g c -> p (g c)")
                    pe.matmul(bR[:, 0:G * CODES], rest_h[:, :], pair_hot, start=False, stop=False,
                              skip_group_check=True)
                    pe.matmul(bR[:, 0:CODES], ones_h[:, :], pair_hot[:, CODES:2 * CODES], start=False, stop=False,
                              skip_group_check=True).then_inc(rank_base_done, 1)
                if 5 in live:
                    q = i - 5
                    pe.wait_ge(hot_ready, q + 1)
                    pair_hot = hot[:, bass.ts(q, G), :].rearrange("p g c -> p (g c)")
                    pe.matmul(bR[:, 0:G * CODES], before_h[:, :], pair_hot, start=False,
                              stop=False, skip_group_check=True)
                    pe.matmul(bR[:, CODES:2 * CODES], ones_h[:, :], pair_hot[:, 0:CODES], start=False, stop=False,
                              skip_group_check=True).then_inc(rank_done, 1)
                if 4 in live:
                    q, b = i - 4, k % 2
                    pe.wait_ge(h1T_ready, q + 1)
                    for g in range(G):
                        mm = pe.matmul(bO[:, G * D + g * E:G * D + (g + 1) * E], h1T[:, b, g, :], rw[:, :],
                                       start=True, stop=True)
                    mm.then_inc(router_done, 1)
            skewed(pe, NP, UNROLL, [1, 2, 4, 5, 6], body)

            pe.wait_ge(diff_ready, NP)

            def group(i, k):
                pe.wait_ge(tile_hot_ready, i + 1)
                pe.wait_ge(place_hot_ready, i + 1)
                for n in range(BG):
                    first, last = (isinstance(i, int) and i == at and n == at * (BG - 1) // (B // BG - 1)
                                   for at in (0, B // BG - 1))
                    mm = pe.matmul(bO[:, 0:TILES], is_place[:, k, n, :], is_tile[:, k, n, :], start=first, stop=last,
                                   skip_group_check=True)
                mm.then_inc(hots_used, 1)
            for i in range(PD):
                group(i, i)
            with pe.Fori(1, B // BG // PD - 1) as turn:
                for k in range(PD):
                    group(turn * PD + k, k)
            for i in range(B // BG - PD, B // BG):
                group(i, i % PD)
            pe.wait_ge(tile_codes_final, 1)
            pe.matmul(bP[0:1, 0:128], tile_code[:, :], ident[:, :], start=True, stop=True).then_inc(tile_row_done, 1)

            pe.wait_ge(experts_in, 16 * 3 * E)
            pe.wait_ge(plan_ready, 1)

            registers = [pe.alloc_register(f"pe_expert{n}") for n in range(2 * TG)]

            def up(dst, w, xt):
                for s in range(HH):
                    mm = pe.matmul(dst[:, s * 128:(s + 1) * 128], w[:, s * 128:(s + 1) * 128], xt, start=True, stop=True)
                return mm

            def down(dst, hT, e):
                for s in range(HH):
                    pe.matmul(dst, hT[:, s, :], We[:, bass.ds(e, 1), UP + s * D:UP + (s + 1) * D], start=s == 0, stop=False)
                return pe.matmul(dst, ones_h[0:3, :], b2s[:, bass.ds(e, 1), :], start=False, stop=True)

            def unit(i, k, live):
                pe.load(registers, plan[0:1, bass.ds(i, 1), 2:4, :].rearrange("p u n g -> p (u n g)"))
                e = [pe.snap(r, min_val=0, max_val=E - 1) for r in registers]
                if 3 in live:
                    u, r = i - 3, (k - 3) % RING
                    for g in range(TG):
                        pe.wait_ge(gathered[r * TG + g], (u - r) * (16 // RING) + 16)
                        mm = pe.transpose(bT[:, g * 128:(g + 1) * 128], tok[:, r, g, 0:D], ident[:, :])
                    mm.then_inc(records_transposed, 1)
                if 4 in live:
                    u, b = i - 4, (k - 4) % 2
                    free(pe, mixed_ready, 1, u, 1)
                    pe.wait_ge(hid1_ready, u + 1)
                    for g in range(TG):
                        mm = down(bP[:, g * D:(g + 1) * D], hid1[:, b, g], e[g])
                    mm.then_inc(out1_done, 1)
                if 3 in live:
                    u, b = i - 3, (k - 3) % 2
                    pe.wait_ge(recordsT_ready, u + 1)
                    for g in range(TG):
                        mm = up(bC[:, g * H:(g + 1) * H], w_up1[:, b, g, :], h1t[:, b, g, :])
                    mm.then_inc(up1_done, 1)
                if 4 in live:
                    u, b = i - 4, (k - 4) % 2
                    pe.wait_ge(boost_ready, u + 1)
                    for g in range(TG):
                        mm = pe.transpose(bZ[:, g * 128:(g + 1) * 128], boost[:, b, g, :], ident[:, :])
                    mm.then_inc(boostT_done, 1)
                if 5 in live:
                    u, b = i - 5, (k - 5) % 2
                    free(pe, z_ready, TG, u, 1)
                    pe.wait_ge(hid2_ready, u + 1)
                    for g in range(TG):
                        mm = down(bR[:, g * D:(g + 1) * D], hid2[:, b, g], e[TG + g])
                    mm.then_inc(out2_done, 1)
                if 4 in live:
                    u, b = i - 4, (k - 4) % 2
                    pe.wait_ge(boostT_ready, u + 1)
                    for g in range(TG):
                        mm = up(bO[:, g * H:(g + 1) * H], w_up2[:, b, g, :], boostt[:, b, g, :])
                    mm.then_inc(up2_done, 1)
            skewed(pe, UNITS, RING, [3, 4, 5], unit)

        @block.scalar
        def _(act):
            for dst, src in ((qw, q_w), (kw, k_w), (gw, gate_w)):
                act.dma_start(dst[:, :], src).then_inc(attention_weights_in, 16)

            def body(i, k, live):
                if isinstance(i, int) and i == 1:
                    act.wait_ge(setup_products_done, 1)
                    act.activation(score_m[:, :], bL[:, 0:128], ACT.Copy, scale=D ** -0.5)
                    act.activation(gwT[:, :], bL[:, 128:256], ACT.Copy).then_inc(setup_weights_ready, 1)
                if 4 in live:
                    q, r, b = i - 4, k % 4, k % 2
                    act.wait_ge(shift1_ready, q + 1)
                    for g in range(G):
                        a = act.activation(rec[:, r, g, 0:D], x1[:, b, g, :], ACT.Identity,
                                           bias=shift1[:, b, g:g + 1], scale=scale1[:, b, g:g + 1])
                    a.then_inc(h1_ready, 1)
                if 1 in live:
                    q, b = i - 1, (k - 1) % 2
                    act.wait_ge(tokens_transposed, q + 1)
                    act.activation(tT[:, b].rearrange("p a g s -> p (a g s)"), bT[:, :], ACT.Copy).then_inc(tT_ready, 1)
                if 2 in live:
                    q, b = i - 2, k % 2
                    act.wait_ge(max_ready, q + 1)
                    for g in range(G):
                        a = act.activation(prob[:, b, g, :], bL[:, g * 256:g * 256 + T], ACT.Exp,
                                           bias=negmax[:, b, g:g + 1], accum_out=denom[:, b, g:g + 1])
                    a.then_inc(prob_ready, 1)
                if 4 in live:
                    q, b = i - 4, k % 2
                    act.wait_ge(h1_transposed, q + 1)
                    act.activation(h1T[:, b].rearrange("p g s -> p (g s)"), bH[:, 0:G * S], ACT.Copy).then_inc(h1T_ready, 1)
                if 1 in live:
                    q, b = i - 1, (k - 1) % 2
                    act.wait_ge(scoremix_done, q + 1)
                    act.activation(cA[:, b, :], bC[:, 0:G * SC + G * S], ACT.Copy).then_inc(cA_ready, 1)
                if 2 in live:
                    q, r = i - 2, (k - 2) % 4
                    act.wait_ge(gate_done, q + 1)
                    act.activation(tanh_z[:, r].rearrange("p g d -> p (g d)"), bZ[:, 0:G * D], ACT.Tanh).then_inc(tanh_ready, 1)
                if 2 in live:
                    q, b = i - 2, k % 2
                    act.wait_ge(prob_transposed, q + 1)
                    act.activation(pTs[:, b].rearrange("p g s -> p (g s)"), bP[:, 0:G * S], ACT.Copy, scale=0.5)
                    act.activation(pTc[:, b].rearrange("p g s -> p (g s)"), bP[0:SC, G * S:2 * G * S],
                                   ACT.Copy, scale=0.5).then_inc(pT_ready, 1)
                if 0 in live:
                    q, r, b = i, k, k % 2
                    act.wait_ge(shift_ready, q + 1)
                    for g in range(G):
                        for n, dst in enumerate((normed[:, b, g, :], h0_half[:, r, g, :])):
                            a = act.activation(dst, x_in[:, r, g, :], ACT.Identity,
                                               bias=shift[:, b, n, g:g + 1], scale=scale[:, b, n, g:g + 1])
                    a.then_inc(tokens_normed, 1)
                if 5 in live:
                    q, b = i - 5, (k - 5) % 2
                    act.wait_ge(ldiff_ready, q + 1)
                    act.activation(lexp[:, b].rearrange("p g e -> p (g e)"), ldiff[:, b].rearrange("p g e -> p (g e)"),
                                   ACT.Exp).then_inc(lexp_ready, 1)
            skewed(act, NP, UNROLL, [0, 1, 2, 4, 5], body)

            act.wait_ge(places_ready, 1)

            def group(i, k):
                free(act, hots_used, 1, i, PD)
                for n in range(BG - 1):
                    a = act.activation(distance[:, k, n, :], codes_f[:, :], ACT.Square, scale=-1.0,
                                       bias=place[:, bass.ds(i * BG + n, 1)])
                a.then_inc(distance_ready, 1)
                act.wait_ge(distance_ready, i + 1)
                act.activation(is_place[:, k, 0:BG - 1, :].rearrange("p n c -> p (n c)"),
                               distance[:, k].rearrange("p n c -> p (n c)"), ACT.Relu, scale=-1.0,
                               bias=ones_f[:, 0:1]).then_inc(place_hot_ready, 1)
            for i in range(PD):
                group(i, i)
            with act.Fori(1, B // BG // PD) as turn:
                for k in range(PD):
                    group(turn * PD + k, k)

            act.wait_ge(experts_in, 16 * 3 * E)
            act.wait_ge(plan_ready, 1)

            registers = [act.alloc_register(f"act_expert{n}") for n in range(2 * TG)]

            def weights(dst, e):
                return act.activation(dst, We[:, bass.ds(e, 1), 0:UP], ACT.Copy)

            def unit(i, k, live):
                act.load(registers, plan[0:1, bass.ds(i + 1, 1), 0:2, :].rearrange("p u n g -> p (u n g)"))
                e = [act.snap(r, min_val=0, max_val=E - 1) for r in registers]
                if 3 in live:
                    u, b = i - 3, (k - 3) % 2
                    act.wait_ge(records_transposed, u + 1)
                    act.activation(h1t[:, b].rearrange("p g t -> p (g t)"), bT[:, 0:TG * 128], ACT.Copy).then_inc(recordsT_ready, 1)
                if 2 in live:
                    b = k % 2
                    free(act, hid1_ready, 1, i - 2, 2)
                    for g in range(TG):
                        weights(w_up1[:, b, g, :], e[g])
                if 4 in live:
                    u, b = i - 4, (k - 4) % 2
                    act.wait_ge(boostT_done, u + 1)
                    act.activation(boostt[:, b].rearrange("p g t -> p (g t)"), bZ[:, 0:TG * 128], ACT.Copy).then_inc(boostT_ready, 1)
                if 3 in live:
                    u, b = i - 3, (k - 3) % 2
                    act.wait_ge(up1_done, u + 1)
                    for g in range(TG):
                        for n in range(HH):
                            at = (g * HH + n) * 128
                            a = act.activation(hid1[:, b, g, n, :], bC[:, at:at + 128], ACT.Relu,
                                               bias=w_up1[:, b, g, H + n:H + n + 1])
                    a.then_inc(hid1_ready, 1)
                if 3 in live:
                    b = (k - 3) % 2
                    free(act, hid2_ready, 1, i - 3, 2)
                    for g in range(TG):
                        weights(w_up2[:, b, g, :], e[TG + g])
            skewed(act, UNITS, RING, [2, 3, 4], unit)

        @block.vector
        def _(dve):
            def body(i, k, live):
                if 2 in live:
                    q, b = i - 2, k % 2
                    dve.wait_ge(scores_done, q + 1)
                    dve.tensor_reduce(negmax[:, b, :], bL[:, :].rearrange("p (g t) -> p g t", g=G)[:, :, 0:T],
                                      AX_X, ALU.max, negate=True).then_inc(max_ready, 1)
                if 0 in live:
                    q, r = i, k
                    dve.wait_ge(x_ready[r], (q - r) * 8 + 32)
                    for g in range(G):
                        v = dve.bn_stats(stats[:, g, :], x_in[:, r, g, :])
                    v.then_inc(stats_ready, 1)
                if 4 in live:
                    q, b = i - 4, k % 2
                    dve.wait_ge(scale1_ready, q + 1)
                    dve.scalar_tensor_tensor(shift1[:, b, :], mv1[:, b, :, 0], -1.0, scale1[:, b, :],
                                             ALU.mult, ALU.mult).then_inc(shift1_ready, 1)
                if 1 in live:
                    q, r = i - 1, (k - 1) % 4
                    dve.wait_ge(tokens_normed, q + 1)
                    dve.scalar_tensor_tensor(xh[:, r, :, :], h0_half[:, r, :, :], 2.0, x_in[:, r, :, :],
                                             ALU.mult, ALU.add).then_inc(xh_ready, 1)
                if 0 in live:
                    dve.wait_ge(stats_ready, i + 1)
                    if 3 not in live:
                        dve.nop(nofuse=True)
                if 3 in live:
                    q, b = i - 3, (k - 3) % 2
                    if 0 not in live:
                        dve.wait_ge(prob_ready, q + 1)
                    dve.reciprocal(rden[:, :], denom[:, b, :]).then_inc(rden_ready, 1)
                if 5 in live:
                    q = i - 5
                    dve.wait_ge(router_done, q + 1)
                    dve.tensor_tensor(lg[:, :, :], bO[:, G * D:G * D + G * E].rearrange("p (g e) -> p g e", g=G),
                                      rb_bc[:, :, :], ALU.add).then_inc(lg_ready, 1)
                if 0 in live:
                    q, b = i, k % 2
                    for g in range(G):
                        v = dve.bn_aggr(mv[:, b, g, :], stats[:, g, :])
                    v.then_inc(mv_ready, 1)
                if 6 in live:
                    q = i - 6
                    dve.wait_ge(rank_done, q + 1)
                    dve.tensor_tensor(hotR[:, :, :], bR[:, 0:G * CODES].rearrange("p (g c) -> p g c", g=G),
                                      hot[:, bass.ts(q, G), :], ALU.mult).then_inc(hotR_ready, 1)
                if 0 in live:
                    q, b = i, k % 2
                    dve.wait_ge(mv_ready, q + 1)
                    dve.tensor_scalar(var_ab[:, b, 0, :], mv[:, b, :, 1], 1.0 + EPS_RMS, EPS_RMS * EPS_LN,
                                      ALU.mult, ALU.add)
                    dve.tensor_scalar(var_ab[:, b, 1, :], mv[:, b, :, 1], EPS_LN, 4.0, ALU.add, ALU.mult).then_inc(var_ready, 1)
                if 3 in live:
                    q, r, b = i - 3, (k - 3) % 4, (k - 3) % 2
                    dve.wait_ge(attended, q + 1)
                    dve.wait_ge(rden_ready, q + 1)
                    for g in range(G):
                        v = dve.scalar_tensor_tensor(diff[:, g, :], bO[:, g * D:(g + 1) * D], rden[:, g:g + 1],
                                                     h0_half[:, r, g, :], ALU.mult, ALU.subtract)
                    v.then_inc(diff_ready, 1)
                if 6 in live:
                    q, b = i - 6, k % 2
                    dve.wait_ge(hotR_ready, q + 1)
                    dve.tensor_reduce(rank[:, bass.ts(q, G)], hotR[:, :, :], AX_X, ALU.add).then_inc(rank_ready, 1)
                    dve.wait_ge(lexp_ready, q + 1)
                    dve.tensor_reduce(lsum[:, :], lexp[:, b, :, :], AX_X, ALU.add).then_inc(lsum_ready, 1)
                if 3 in live:
                    q, r, b = i - 3, (k - 3) % 4, (k - 3) % 2
                    dve.wait_ge(tanh_ready, q + 1)
                    dve.wait_ge(diff_ready, q + 1)
                    dve.scalar_tensor_tensor(gated[:, b, :, :], tanh_z[:, r, :, :], 1.0, diff[:, :, :],
                                             ALU.add, ALU.mult).then_inc(gated_ready, 1)
                if 5 in live:
                    q, b = i - 5, (k - 5) % 2
                    dve.wait_ge(lg_ready, q + 1)
                    dve.nop(nofuse=True)
                    for g in range(G):
                        v = dve.max(top[:, g, :], lg[:, g, :])
                    v.then_inc(top_ready, 1)
                if 6 in live:
                    q, r = i - 6, (k - 6) % 4
                    dve.wait_ge(lsum_ready, q + 1)
                    dve.reciprocal(rec[:, r, :, 2 * D:2 * D + 1], lsum[:, :].unsqueeze(2)).then_inc(weight1_ready, 1)
                if 5 in live:
                    q, b = i - 5, (k - 5) % 2
                    dve.wait_ge(top_ready, q + 1)
                    dve.tensor_tensor(ldiff[:, b, :, :], top[:, :, :], top[:, :, 0:1].to_broadcast([128, G, E]),
                                      ALU.subtract).then_inc(ldiff_ready, 1)
                    for g in range(G):
                        v = dve.max_index(topi[:, g, :], top[:, g, :], lg[:, g, :])
                    v.then_inc(topi_ready, 1)
                if 6 in live:
                    q, r, b = i - 6, (k - 6) % 4, k % 2
                    dve.wait_ge(weight1_ready, q + 1)
                    dve.tensor_tensor(rec[:, r, :, 2 * D + 1:2 * D + 2], rec[:, r, :, 2 * D:2 * D + 1],
                                      lexp[:, b, :, 1:2], ALU.mult).then_inc(weights_ready, 1)
                if 0 in live:
                    q, b = i, k % 2
                    dve.wait_ge(scales_ready, q + 1)
                    dve.scalar_tensor_tensor(shift[:, b, :, :], mv[:, b, :, 0].unsqueeze(1).to_broadcast([128, 2, G]), -1.0,
                                             scale[:, b, :, :], ALU.mult, ALU.mult).then_inc(shift_ready, 1)
                if 5 in live:
                    q = i - 5
                    dve.wait_ge(topi_ready, q + 1)
                    dve.scalar_tensor_tensor(code[:, bass.ts(q, G)], topi[:, :, 0], float(E), topi[:, :, 1],
                                             ALU.mult, ALU.add).then_inc(code_ready, 1)
                if 5 in live:
                    q = i - 5
                    dve.wait_ge(code_ready, q + 1)
                    dve.tensor_tensor(hot[:, bass.ts(q, G), :], codes_f[:, 0:CODES].unsqueeze(1).to_broadcast([128, G, CODES]),
                                      code[:, bass.ts(q, G)].unsqueeze(2).to_broadcast([128, G, CODES]),
                                      ALU.is_equal).then_inc(hot_ready, 1)
                if 3 in live:
                    q, b = i - 3, (k - 3) % 2
                    dve.wait_ge(x1_ready, q + 1)
                    for g in range(G):
                        v = dve.bn_stats(stats1[:, g, :], x1[:, b, g, :])
                    v.then_inc(stats1_ready, 1)
                    dve.wait_ge(stats1_ready, q + 1)
                    dve.nop(nofuse=True)
                    for g in range(G):
                        v = dve.bn_aggr(mv1[:, b, g, :], stats1[:, g, :])
                    v.then_inc(mv1_ready, 1)
                    dve.wait_ge(mv1_ready, q + 1)
                    dve.tensor_scalar(var1[:, b, :], mv1[:, b, :, 1], EPS_LN, None, ALU.add).then_inc(var1_ready, 1)
                if isinstance(i, int) and i == 0:
                    split_biases()

            def split_biases():
                dve.wait_ge(biases_in, 32)
                dve.tensor_scalar(bias_col[:, BC - 1:BC], bias_col[:, BC - 1:BC], 0.5, None, ALU.mult).then_inc(bias_step_done, 1)
                dve.wait_ge(bias_step_done, 1)
                dve.tensor_copy(bias_parts[:, 0, :], bias_col[:, :]).then_inc(bias_step_done, 1)
                dve.wait_ge(bias_step_done, 2)
                dve.tensor_tensor(rest1[:, :], bias_col[:, :], bias_parts[:, 0, :], ALU.subtract).then_inc(bias_step_done, 1)
                dve.wait_ge(bias_step_done, 3)
                dve.tensor_copy(bias_parts[:, 1, :], rest1[:, :]).then_inc(bias_step_done, 1)
                dve.wait_ge(bias_step_done, 4)
                dve.tensor_tensor(rest2[:, :], rest1[:, :], bias_parts[:, 1, :], ALU.subtract).then_inc(bias_step_done, 1)
                dve.wait_ge(bias_step_done, 5)
                dve.tensor_copy(bias_parts[:, 2, :], rest2[:, :]).then_inc(bias_parts_ready, 1)

            skewed(dve, NP, UNROLL, [0, 1, 2, 3, 4, 5, 6], body)

            dve.wait_ge(rank_base_done, NP)
            dve.wait_ge(constants_ready, 3)
            dve.wait_ge(rank_ready, NP)
            dve.tensor_scalar(count_i[:, :], bR[:, 0:CODES], 127.0, None, ALU.add)
            dve.tensor_copy(rank_i[:, :], rank[:, :])
            dve.tensor_copy(token_f[:, :], token_i[:, :])
            dve.tensor_copy(part_f[:, :], part_i[:, :]).then_inc(counts_ready, 1)
            dve.wait_ge(counts_ready, 1)
            dve.tensor_scalar(rank_lo[:, :], rank_i[:, :], 127, None, ALU.bitwise_and)
            dve.tensor_scalar(rank_hi[:, :], rank_i[:, :], 7, None, ALU.logical_shift_right)
            dve.tensor_scalar(tiles_i[:, :], count_i[:, :], 7, None, ALU.logical_shift_right).then_inc(tiles_ready, 1)
            dve.wait_ge(tiles_ready, 1)
            dve.tensor_copy(place[:, :], rank_lo[:, :]).then_inc(places_ready, 1)
            dve.tensor_copy(tiles_f[:, :], tiles_i[:, :]).then_inc(tiles_f_ready, 1)
            dve.wait_ge(tiles_f_ready, 1)
            dve.tensor_tensor_scan(tile_end[:, :], ones_f[:, :], tiles_f[:, :], 0.0, ALU.mult, ALU.add).then_inc(tile_end_ready, 1)
            dve.wait_ge(tile_end_ready, 1)
            dve.tensor_tensor(start_h[:, :], tile_end[:, :], tiles_f[:, :], ALU.subtract).then_inc(starts_ready, 1)
            dve.tensor_scalar(ended[:, :], tile_end[:, :], part_f[:, 0:1], None, ALU.is_le).then_inc(ended_ready, 1)
            dve.wait_ge(starts_ready, 1)
            dve.tensor_tensor(hot_start[:, :, :], hot[:, :, :],
                              start_h[:, :].unsqueeze(1).to_broadcast([128, 64, CODES]), ALU.mult).then_inc(hot_start_ready, 1)
            dve.wait_ge(ended_ready, 1)
            dve.tensor_reduce(tile_code[:, :], ended[:, :], AX_X, ALU.add).then_inc(tile_code_ready, 1)
            half = CODES
            source = hot_start
            step = 0
            for target in (half1, half2, half3):
                half //= 2
                step += 1
                dve.wait_ge(hot_start_ready, step)
                dve.tensor_tensor(target[:, :, :], source[:, :, 0:half], source[:, :, half:2 * half], ALU.add).then_inc(hot_start_ready, 1)
                source = target
            dve.wait_ge(tile_code_ready, 1)
            dve.tensor_scalar(tile_code[:, :], tile_code[:, :], float(CODES - 1), None, ALU.min).then_inc(tile_codes_final, 1)
            dve.wait_ge(hot_start_ready, step + 1)
            dve.tensor_reduce(start_of[:, :], source[:, :, :], AX_X, ALU.add).then_inc(start_of_ready, 1)
            dve.wait_ge(start_of_ready, 1)
            dve.tensor_tensor(tile_of[:, :], start_of[:, :], rank_hi[:, :], ALU.add).then_inc(tile_of_ready, 1)
            dve.wait_ge(tile_of_ready, 1)

            def group(i, k):
                free(dve, hots_used, 1, i, PD)
                n = BG - 1
                dve.tensor_scalar(is_place[:, k, n, :], codes_f[:, :], place[:, bass.ds(i * BG + n, 1)], None, ALU.is_equal)
                for n in range(BG):
                    v = dve.tensor_scalar(is_tile[:, k, n, :], codes_f[:, 0:TILES], tile_of[:, bass.ds(i * BG + n, 1)],
                                          token_f[:, bass.ds(i * BG + n, 1)], ALU.is_equal, ALU.mult)
                v.then_inc(tile_hot_ready, 1)
            for i in range(PD):
                group(i, i)
            with dve.Fori(1, B // BG // PD) as turn:
                for k in range(PD):
                    group(turn * PD + k, k)

            dve.wait_ge(hots_used, B // BG)
            dve.tensor_scalar(empty[:, :], bO[:, 0:TILES], 0.5, SKIPPED, ALU.is_lt, ALU.mult)
            dve.tensor_scalar(gather_at[:, :], bO[:, 0:TILES], -1.0, 0.0, ALU.add, ALU.max)
            dve.tensor_copy(slots[:, :], bO[:, 0:TILES]).then_inc(slots_ready, 1)
            dve.wait_ge(slots_ready, 1)
            dve.scalar_tensor_tensor(scatter_at[:, :], slots[:, :], -1.0, empty[:, :], ALU.add, ALU.add).then_inc(slot_tables_ready, 1)
            dve.wait_ge(tile_row_done, 1)
            dve.tensor_copy(tile_row[:, :], bP[0:1, 0:128]).then_inc(tile_row_ready, 1)
            dve.wait_ge(tile_row_ready, 1)
            for n, lag, op, by in ((0, 3, ALU.logical_shift_right, 3), (1, 4, ALU.bitwise_and, E - 1),
                                   (2, 4, ALU.logical_shift_right, 3), (3, 5, ALU.bitwise_and, E - 1)):
                v = dve.tensor_scalar(plan[:, lag:lag + UNITS, n, :],
                                      tile_row[:, 0:TILES].rearrange("p (u g) -> p u g", g=TG), by, None, op)
            v.then_inc(plan_ready, 1)

            dve.wait_ge(slot_tables_ready, 1)

            def unit(i, k, live):
                if 0 in live:
                    u, r = i, k
                    if k % 2 == 0:
                        free(dve, records_transposed, 1, u, RING - 1)
                        dve.tensor_copy(gather_now[:, r * TG:(r + 2) * TG],
                                        gather_at[:, bass.ds(u * TG, 2 * TG)]).then_inc(gather_cols, 2)
                if 4 in live:
                    u, r, b = i - 4, (k - 4) % RING, (k - 4) % 2
                    dve.wait_ge(out1_done, u + 1)
                    dve.scalar_tensor_tensor(boost[:, b], bP[:, 0:TG * D].rearrange("p (g d) -> p g d", g=TG), 0.5,
                                             tok[:, r, :, 0:D], ALU.mult, ALU.add).then_inc(boost_ready, 1)
                    for g in range(TG):
                        v = dve.scalar_tensor_tensor(mixed[:, b, g, :], bP[:, g * D:(g + 1) * D], tok[:, r, g, 2 * D:2 * D + 1],
                                                     tok[:, r, g, 0:D], ALU.mult, ALU.add)
                    v.then_inc(mixed_ready, 1)
                if 6 in live:
                    u, r, b, o = i - 6, (k - 6) % RING, k % 2, (k - 6) % ROWS
                    if r % 2 == 0:
                        dve.tensor_copy(scatter_now[:, r * TG:(r + 2) * TG],
                                        scatter_at[:, bass.ds(u * TG, 2 * TG)]).then_inc(scatter_cols, 1)
                    dve.wait_ge(scalez_ready, u + 1)
                    for g in range(TG):
                        v = dve.scalar_tensor_tensor(y[:, g, :], z[:, b, g, :], mvz[:, b, g, 0:1], gamma_bc[:, :],
                                                     ALU.subtract, ALU.mult)
                    v.then_inc(y_ready, 1)
                    dve.wait_ge(y_ready, u + 1)
                    for g in range(TG):
                        if not (isinstance(u, int) and u < ROWS):
                            dve.wait_ge(scattered[o * TG + g], (u - o) * (16 // ROWS))
                        v = dve.scalar_tensor_tensor(row_out[:, o, g, :], y[:, g, :], scalez[:, b, g:g + 1], tok[:, r, g, D:2 * D],
                                                     ALU.mult, ALU.add)
                    v.then_inc(rows_ready, 1)
                if 5 in live:
                    u, r, b = i - 5, (k - 5) % RING, (k - 5) % 2
                    dve.wait_ge(out2_done, u + 1)
                    for g in range(TG):
                        dve.scalar_tensor_tensor(z[:, b, g, :], bR[:, g * D:(g + 1) * D], tok[:, r, g, 2 * D + 1:2 * D + 2],
                                                 mixed[:, b, g, :], ALU.mult, ALU.add).then_inc(z_ready, 1)
                    for g in range(TG):
                        dve.wait_ge(z_ready, TG * u + g + 1)
                        dve.bn_stats(statsz[:, b, g, :], z[:, b, g, :]).then_inc(zstats_ready, 1)
                    dve.wait_ge(zstats_ready, TG * (u + 1))
                    dve.nop(nofuse=True)
                    for g in range(TG):
                        v = dve.bn_aggr(mvz[:, b, g, :], statsz[:, b, g, :])
                    v.then_inc(zmv_ready, 1)
                    dve.wait_ge(zmv_ready, u + 1)
                    dve.tensor_scalar(varz[:, b, :], mvz[:, b, :, 1], EPS_LN, None, ALU.add).then_inc(varz_ready, 1)
                if 4 in live:
                    u, b = i - 4, (k - 4) % 2
                    dve.wait_ge(up2_done, u + 1)
                    for g in range(TG):
                        for n in range(HH):
                            at = (g * HH + n) * 128
                            v = dve.tensor_scalar(hid2[:, b, g, n, :], bO[:, at:at + 128], w_up2[:, b, g, H + n:H + n + 1],
                                                  0.0, ALU.add, ALU.max)
                    v.then_inc(hid2_ready, 1)
            skewed(dve, UNITS, RING, [0, 4, 5, 6], unit)
            dve.wait_ge(scatter_cols, UNITS // 2)


_INS = ["x", "ctx_1024", "L0_xattn_q_w", "L0_xattn_k_w", "L0_xattn_norm_w", "L0_xattn_gate_w", "L0_xattn_gate_b",
        "L0_ffn_gate_W", "L0_ffn_gate_b", "L0_ffn_W1", "L0_ffn_b1", "L0_ffn_W2", "L0_ffn_b2", "L0_ffn_ln_gamma",
        "L0_ffn_ln_beta"]
_OUTS = [((B, S, D), "float32")]


def kernel(**inputs):
    import numpy as np
    import concourse.bacc as bacc
    from concourse.bass_utils import run_bass_kernel_spmd

    nc = bacc.Bacc("TRN2", target_bir_lowering=False, num_devices=1)
    arrays, args = {}, []
    for name in _INS:
        a = np.ascontiguousarray(inputs[name])
        arrays[f"in_{name}_dram"] = a
        args.append(nc.dram_tensor(f"in_{name}_dram", a.shape, mybir.dt.from_np(a.dtype), kind="ExternalInput").ap())
    for n, (shape, dtype) in enumerate(_OUTS):
        args.append(nc.dram_tensor(f"out_{n}_dram", shape, mybir.dt.from_np(np.dtype(dtype)), kind="ExternalOutput").ap())
    program(nc, *args)
    r = run_bass_kernel_spmd(nc, [arrays], core_ids=[0])
    return r.results[0]["out_0_dram"]
```
